# Optimizing a Trainium2 kernel written in Bass

```python
import numpy as np
import jax
import jax.numpy as jnp

def _softmax(x, axis=-1):
    return jax.nn.softmax(x, axis=axis)

def _gelu(x):
    return jax.nn.gelu(x, approximate=True)

def _silu(x):
    return jax.nn.silu(x)

def _sigmoid(x):
    return jax.nn.sigmoid(x)

def _layernorm(x, axis=-1, eps=1e-05):
    m = jnp.mean(x, axis=axis, keepdims=True)
    v = jnp.var(x, axis=axis, keepdims=True)
    return (x - m) / jnp.sqrt(v + eps)

def _scatter_add(tgt, idx, src, axis=0):
    return tgt.at[idx].add(src)

def _segment_sum(src, seg, n):
    return jax.ops.segment_sum(src, seg, n)
kernel_name = 'mk_flamingo_gated_d2_seqx_r4_2bf7c9'

def setup_inputs(seed: int=0):
    np.random.seed(seed)
    _w = jnp.asarray

    def _rec_inputs():
        import jax
        import jax.numpy as jnp
        _rk = jax.random.key(seed)
        x = -0.0002928 + 1 * jax.random.normal(jax.random.fold_in(_rk, 1), (32, 112, 256), jnp.float32)
        _lenS = 112 - jax.random.randint(jax.random.fold_in(_rk, 7), (32,), 0, max(1, 112 // 4) + 1, jnp.int32)
        _lenS2 = 375 - jax.random.randint(jax.random.fold_in(_rk, 8), (32,), 0, max(1, 375 // 4) + 1, jnp.int32)
        _ctx_1024P = jax.random.normal(jax.random.fold_in(_rk, 11), (32, 16, 256), jnp.float32)
        _ctx_1024c = jax.random.dirichlet(jax.random.fold_in(_rk, 511), 0.3 * jnp.ones((16,), jnp.float32), (32, 375))
        _ctx_1024t = jnp.einsum('bsk,bkd->bsd', _ctx_1024c, _ctx_1024P)
        _ctx_1024t = _ctx_1024t * jax.lax.rsqrt(jnp.mean(jnp.square(_ctx_1024t)) + 1e-12) * 0.953939
        ctx_1024 = -1.39393e-06 + 0.999914 * (_ctx_1024t + 0.3 * jax.random.normal(jax.random.fold_in(_rk, 611), (32, 375, 256), jnp.float32))
        _g = jax.random.normal(jax.random.fold_in(_rk, 9001), (2, 2), jnp.float32)
        _g = jnp.sign(_g) * jnp.maximum(jnp.abs(_g), 1.0) + (_g == 0) * 1.0
        g_xattn = _g[0]
        g_ffn = _g[1]
        return (x, ctx_1024, g_xattn, g_ffn)
    x, ctx_1024, g_xattn, g_ffn = _rec_inputs()

    def _L0_xattn_setup():
        import jax, jax.numpy as jnp
        import numpy as np
        DIM = 256
        HEADS = 16
        HEAD_DIM = DIM // HEADS
        SCALE = HEAD_DIM ** (-0.5)

        def _split_heads(t):
            b, n, _ = t.shape
            return t.reshape(b, n, HEADS, HEAD_DIM).transpose(0, 2, 1, 3)
        key = jax.random.key(seed)
        ks = jax.random.split(key, 7)
        B, N, M = (2, 512, 512)
        x = jax.random.normal(ks[0], (B, N, DIM), dtype=jnp.float32)
        y = jax.random.normal(ks[1], (B, M, DIM), dtype=jnp.float32)
        s = DIM ** (-0.5)
        Wq = jax.random.normal(ks[2], (DIM, DIM), dtype=jnp.float32) * s
        Wk = jax.random.normal(ks[3], (DIM, DIM), dtype=jnp.float32) * s
        Wv = jax.random.normal(ks[4], (DIM, DIM), dtype=jnp.float32) * s
        Wp = jax.random.normal(ks[5], (DIM, DIM), dtype=jnp.float32) * s
        bp = jax.random.normal(ks[6], (DIM,), dtype=jnp.float32) * 0.01
        return {'x': x, 'y': y, 'Wq': Wq, 'Wk': Wk, 'Wv': Wv, 'Wp': Wp, 'bp': bp}
    _L0_xattn_all = _L0_xattn_setup()
    _L0_xattn_in = {k: v for k, v in _L0_xattn_all.items() if k in ('Wq', 'Wk', 'Wv', 'Wp', 'bp')}
    del _L0_xattn_all

    def _L0_ffn_setup():
        import jax, jax.numpy as jnp
        import numpy as np
        B, C, D = (2, 512, 256)
        I = 512
        E, K = (8, 2)
        CF = 1.25
        key = jax.random.key(seed)
        k1, k2, k3, k4 = jax.random.split(key, 4)
        scale = 0.02
        return {'hidden_states': jax.random.normal(k1, (B, C, D), jnp.float32), 'Wg': jax.random.normal(k2, (E, D), jnp.float32) * scale, 'W1': jax.random.normal(k3, (E, D, 2 * I), jnp.float32) * scale, 'W2': jax.random.normal(k4, (E, I, D), jnp.float32) * scale}
    _L0_ffn_all = _L0_ffn_setup()
    _L0_ffn_in = {k: v for k, v in _L0_ffn_all.items() if k in ('Wg', 'W1', 'W2')}
    del _L0_ffn_all

    def _L1_xattn_setup():
        import jax, jax.numpy as jnp
        import numpy as np
        H = 256
        B = 8
        L_CHAR = 512
        L_SUB = 256

        def _linear(x, W, b):
            return jnp.einsum('blh,oh->blo', x, W) + b

        def _interp_linear(x, out_len):
            L_in = x.shape[1]
            pos = (jnp.arange(out_len, dtype=x.dtype) + 0.5) * (L_in / out_len) - 0.5
            pos = jnp.clip(pos, 0.0, L_in - 1)
            lo = jnp.floor(pos).astype(jnp.int32)
            hi = jnp.minimum(lo + 1, L_in - 1)
            w = (pos - lo.astype(x.dtype))[None, :, None]
            return x[:, lo] * (1 - w) + x[:, hi] * w
        key = jax.random.key(seed)
        ks = jax.random.split(key, 18)
        s = 0.02
        inp = {'char_emb': jax.random.normal(ks[0], (B, L_CHAR, H), jnp.float32), 'subword_emb': jax.random.normal(ks[1], (B, L_SUB, H), jnp.float32)}
        names = ['Wq_c', 'Wk_s', 'Wv_s', 'Wq_s', 'Wk_c', 'Wv_c']
        for i, n in enumerate(names):
            inp[n] = jax.random.normal(ks[2 + 2 * i], (H, H), jnp.float32) * s
            inp['b' + n[1:]] = jax.random.normal(ks[3 + 2 * i], (H,), jnp.float32) * s
        inp['Wg'] = jax.random.normal(ks[14], (H, 2 * H), jnp.float32) * s
        inp['bg'] = jax.random.normal(ks[15], (H,), jnp.float32) * s
        return inp
    _L1_xattn_all = _L1_xattn_setup()
    _L1_xattn_in = {k: v for k, v in _L1_xattn_all.items() if k in ('Wq_c', 'bq_c', 'Wk_s', 'bk_s', 'Wv_s', 'bv_s', 'Wq_s', 'bq_s', 'Wk_c', 'bk_c', 'Wv_c', 'bv_c', 'Wg', 'bg')}
    del _L1_xattn_all

    def _L1_ffn_setup():
        import jax, jax.numpy as jnp
        import numpy as np
        B, T, D = (2, 256, 256)
        H, DK, K = (8, 128, 8)
        NKEYS = 64
        NEXP = NKEYS * NKEYS

        def _rmsnorm(x, w, eps=1e-06):
            inv = jax.lax.rsqrt(jnp.mean(x * x, axis=-1, keepdims=True) + eps)
            return x * inv * w
        key = jax.random.key(seed)
        ks = jax.random.split(key, 5)
        return {'x': jax.random.normal(ks[0], (B, T, D), jnp.float32), 'w_q': jax.random.normal(ks[1], (H * 2 * DK, D), jnp.float32) * 0.02, 'keys': jax.random.normal(ks[2], (H, NKEYS, 2, DK), jnp.float32) * 0.02, 'expert_down': jax.random.normal(ks[3], (NEXP, D), jnp.float32) * 0.02, 'expert_up': jax.random.normal(ks[4], (NEXP, D), jnp.float32) * 0.02, 'norm_w': jnp.ones((D,), jnp.float32)}
    _L1_ffn_all = _L1_ffn_setup()
    _L1_ffn_in = {k: v for k, v in _L1_ffn_all.items() if k in ('w_q', 'keys', 'expert_down', 'expert_up', 'norm_w')}
    del _L1_ffn_all
    return {'x': x, 'ctx_1024': ctx_1024, 'g_xattn': g_xattn, 'g_ffn': g_ffn, 'L0_xattn_Wq': _L0_xattn_in['Wq'], 'L0_xattn_Wk': _L0_xattn_in['Wk'], 'L0_xattn_Wv': _L0_xattn_in['Wv'], 'L0_xattn_Wp': _L0_xattn_in['Wp'], 'L0_xattn_bp': _L0_xattn_in['bp'], 'L0_ffn_Wg': _L0_ffn_in['Wg'], 'L0_ffn_W1': _L0_ffn_in['W1'], 'L0_ffn_W2': _L0_ffn_in['W2'], 'L1_xattn_Wq_c': _L1_xattn_in['Wq_c'], 'L1_xattn_bq_c': _L1_xattn_in['bq_c'], 'L1_xattn_Wk_s': _L1_xattn_in['Wk_s'], 'L1_xattn_bk_s': _L1_xattn_in['bk_s'], 'L1_xattn_Wv_s': _L1_xattn_in['Wv_s'], 'L1_xattn_bv_s': _L1_xattn_in['bv_s'], 'L1_xattn_Wq_s': _L1_xattn_in['Wq_s'], 'L1_xattn_bq_s': _L1_xattn_in['bq_s'], 'L1_xattn_Wk_c': _L1_xattn_in['Wk_c'], 'L1_xattn_bk_c': _L1_xattn_in['bk_c'], 'L1_xattn_Wv_c': _L1_xattn_in['Wv_c'], 'L1_xattn_bv_c': _L1_xattn_in['bv_c'], 'L1_xattn_Wg': _L1_xattn_in['Wg'], 'L1_xattn_bg': _L1_xattn_in['bg'], 'L1_ffn_w_q': _L1_ffn_in['w_q'], 'L1_ffn_keys': _L1_ffn_in['keys'], 'L1_ffn_expert_down': _L1_ffn_in['expert_down'], 'L1_ffn_expert_up': _L1_ffn_in['expert_up'], 'L1_ffn_norm_w': _L1_ffn_in['norm_w']}

def reference(x, ctx_1024, g_xattn, g_ffn, L0_xattn_Wq, L0_xattn_Wk, L0_xattn_Wv, L0_xattn_Wp, L0_xattn_bp, L0_ffn_Wg, L0_ffn_W1, L0_ffn_W2, L1_xattn_Wq_c, L1_xattn_bq_c, L1_xattn_Wk_s, L1_xattn_bk_s, L1_xattn_Wv_s, L1_xattn_bv_s, L1_xattn_Wq_s, L1_xattn_bq_s, L1_xattn_Wk_c, L1_xattn_bk_c, L1_xattn_Wv_c, L1_xattn_bv_c, L1_xattn_Wg, L1_xattn_bg, L1_ffn_w_q, L1_ffn_keys, L1_ffn_expert_down, L1_ffn_expert_up, L1_ffn_norm_w):
    import jax
    import jax.numpy as jnp

    def _L0_xattn_ref(x, y, Wq, Wk, Wv, Wp, bp):
        import jax, jax.numpy as jnp
        import numpy as np
        DIM = 256
        HEADS = 16
        HEAD_DIM = DIM // HEADS
        SCALE = HEAD_DIM ** (-0.5)

        def _split_heads(t):
            b, n, _ = t.shape
            return t.reshape(b, n, HEADS, HEAD_DIM).transpose(0, 2, 1, 3)
        q = _split_heads(x @ Wq)
        k = _split_heads(y @ Wk)
        v = _split_heads(y @ Wv)
        attn = jnp.einsum('bhid,bhjd->bhij', q, k) * SCALE
        attn = jax.nn.softmax(attn, axis=-1)
        out = jnp.einsum('bhij,bhjd->bhid', attn, v)
        b, h, n, d = out.shape
        out = out.transpose(0, 2, 1, 3).reshape(b, n, h * d)
        return out @ Wp + bp

    def _L0_ffn_ref(hidden_states, Wg, W1, W2):
        import jax, jax.numpy as jnp
        import numpy as np
        B, C, D = (2, 512, 256)
        I = 512
        E, K = (8, 2)
        CF = 1.25
        Bx, Cx, d = hidden_states.shape
        N = Bx * Cx
        cap = int(N * K * CF / E)
        x = hidden_states.reshape(N, d)
        logits = x @ Wg.T
        top_v, top_i = jax.lax.top_k(logits, K)
        gates = jax.nn.softmax(top_v, axis=-1)
        flat_e = top_i.reshape(N * K)
        gates_f = gates.reshape(N * K)
        tok = jnp.repeat(jnp.arange(N), K)
        onehot = jax.nn.one_hot(flat_e, E, dtype=jnp.int32)
        pos = jnp.cumsum(onehot, axis=0) - 1
        pos_f = jnp.take_along_axis(pos, flat_e[:, None], axis=1)[:, 0]
        keep = pos_f < cap
        pos_safe = jnp.where(keep, pos_f, cap)
        exp_batches = jnp.zeros((E, cap, d), x.dtype).at[flat_e, pos_safe].set(x[tok], mode='drop')
        h = jnp.einsum('ecd,edf->ecf', exp_batches, W1)
        inp, gate = jnp.split(h, 2, axis=-1)
        h = jax.nn.gelu(inp, approximate=False) * gate
        exp_out = jnp.einsum('eci,eid->ecd', h, W2)
        gathered = exp_out[flat_e, jnp.minimum(pos_safe, cap - 1)]
        contrib = jnp.where(keep, gates_f, 0.0)[:, None] * gathered
        out = jax.ops.segment_sum(contrib, tok, num_segments=N)
        return out.reshape(Bx, Cx, d)

    def _L1_xattn_ref(char_emb, subword_emb, Wq_c, bq_c, Wk_s, bk_s, Wv_s, bv_s, Wq_s, bq_s, Wk_c, bk_c, Wv_c, bv_c, Wg, bg):
        import jax, jax.numpy as jnp
        import numpy as np
        H = 256
        B = 8
        L_CHAR = 512
        L_SUB = 256

        def _linear(x, W, b):
            return jnp.einsum('blh,oh->blo', x, W) + b

        def _interp_linear(x, out_len):
            L_in = x.shape[1]
            pos = (jnp.arange(out_len, dtype=x.dtype) + 0.5) * (L_in / out_len) - 0.5
            pos = jnp.clip(pos, 0.0, L_in - 1)
            lo = jnp.floor(pos).astype(jnp.int32)
            hi = jnp.minimum(lo + 1, L_in - 1)
            w = (pos - lo.astype(x.dtype))[None, :, None]
            return x[:, lo] * (1 - w) + x[:, hi] * w
        h = char_emb.shape[-1]
        scale = 1.0 / jnp.sqrt(jnp.asarray(h, char_emb.dtype))
        Q_char = _linear(char_emb, Wq_c, bq_c)
        K_sub = _linear(subword_emb, Wk_s, bk_s)
        V_sub = _linear(subword_emb, Wv_s, bv_s)
        scores = jnp.einsum('bqh,bkh->bqk', Q_char, K_sub) * scale
        char2sub = jnp.einsum('bqk,bkh->bqh', jax.nn.softmax(scores, axis=-1), V_sub)
        Q_sub = _linear(subword_emb, Wq_s, bq_s)
        K_char = _linear(char_emb, Wk_c, bk_c)
        V_char = _linear(char_emb, Wv_c, bv_c)
        scores2 = jnp.einsum('bqh,bkh->bqk', Q_sub, K_char) * scale
        sub2char = jnp.einsum('bqk,bkh->bqh', jax.nn.softmax(scores2, axis=-1), V_char)
        L_char = char_emb.shape[1]
        if sub2char.shape[1] != L_char:
            sub2char = _interp_linear(sub2char, L_char)
        gate_in = jnp.concatenate([char2sub, sub2char], axis=-1)
        gate = jax.nn.sigmoid(jnp.einsum('blh,oh->blo', gate_in, Wg) + bg)
        return gate * char2sub + (1 - gate) * sub2char

    def _L1_ffn_ref(x, w_q, keys, expert_down, expert_up, norm_w):
        import jax, jax.numpy as jnp
        import numpy as np
        B, T, D = (2, 256, 256)
        H, DK, K = (8, 128, 8)
        NKEYS = 64
        NEXP = NKEYS * NKEYS

        def _rmsnorm(x, w, eps=1e-06):
            inv = jax.lax.rsqrt(jnp.mean(x * x, axis=-1, keepdims=True) + eps)
            return x * inv * w
        b, t, d = x.shape
        xn = _rmsnorm(x, norm_w)
        q = (xn @ w_q.T).reshape(b, t, H, 2, DK)
        sim1 = jnp.einsum('bthd,hkd->bthk', q[..., 0, :], keys[:, :, 0, :])
        sim2 = jnp.einsum('bthd,hkd->bthk', q[..., 1, :], keys[:, :, 1, :])
        s1, i1 = jax.lax.top_k(sim1, K)
        s2, i2 = jax.lax.top_k(sim2, K)
        all_idx = (i1[..., :, None] * NKEYS + i2[..., None, :]).reshape(b, t, H, K * K)
        all_sc = (s1[..., :, None] + s2[..., None, :]).reshape(b, t, H, K * K)
        fs, pk = jax.lax.top_k(all_sc, K)
        fi = jnp.take_along_axis(all_idx, pk, axis=-1)
        wd = expert_down[fi]
        wu = expert_up[fi]
        hidden = jax.nn.gelu(jnp.einsum('btd,bthkd->bthk', xn, wd), approximate=False)
        hidden = hidden * jax.nn.relu(fs)
        return jnp.einsum('bthk,bthkd->btd', hidden, wu)
    x = x + jnp.tanh(g_xattn[0]) * _L0_xattn_ref(_layernorm(x, axis=-1), ctx_1024, L0_xattn_Wq, L0_xattn_Wk, L0_xattn_Wv, L0_xattn_Wp, L0_xattn_bp)
    x = x + jnp.tanh(g_ffn[0]) * _L0_ffn_ref(_layernorm(x, axis=-1), L0_ffn_Wg, L0_ffn_W1, L0_ffn_W2)
    x = x + jnp.tanh(g_xattn[1]) * _L1_xattn_ref(_layernorm(x, axis=-1), ctx_1024, L1_xattn_Wq_c, L1_xattn_bq_c, L1_xattn_Wk_s, L1_xattn_bk_s, L1_xattn_Wv_s, L1_xattn_bv_s, L1_xattn_Wq_s, L1_xattn_bq_s, L1_xattn_Wk_c, L1_xattn_bk_c, L1_xattn_Wv_c, L1_xattn_bv_c, L1_xattn_Wg, L1_xattn_bg)
    x = x + jnp.tanh(g_ffn[1]) * _L1_ffn_ref(_layernorm(x, axis=-1), L1_ffn_w_q, L1_ffn_keys, L1_ffn_expert_down, L1_ffn_expert_up, L1_ffn_norm_w)
    return x

_drawn_inputs = setup_inputs


def setup_inputs(seed=0):
    import zlib

    import numpy as np

    out = dict(_drawn_inputs(seed))
    spreads = {'g_ffn': (-1.0, 0.6), 'L1_ffn_norm_w': (1.0, 0.6)}
    factors = {'L0_xattn_bp': 7.504,
     'L0_ffn_Wg': 5.207,
     'L0_ffn_W1': 4.541,
     'L0_ffn_W2': 4.528,
     'L1_xattn_Wq_c': 8.0,
     'L1_xattn_bq_c': 8.0,
     'L1_xattn_Wk_s': 8.0,
     'L1_xattn_bk_s': 8.0,
     'L1_xattn_bv_s': 6.377,
     'L1_xattn_Wq_s': 8.0,
     'L1_xattn_bq_s': 8.0,
     'L1_xattn_Wk_c': 8.0,
     'L1_xattn_bk_c': 8.0,
     'L1_xattn_bv_c': 6.168,
     'L1_xattn_Wg': 8.0,
     'L1_xattn_bg': 8.0,
     'L1_ffn_w_q': 7.688,
     'L1_ffn_keys': 7.587,
     'L1_ffn_expert_down': 7.799,
     'L1_ffn_expert_up': 7.518}
    for name, (base, spread) in spreads.items():
        noise = np.random.default_rng([zlib.crc32(name.encode()), seed]).standard_normal(out[name].shape)
        drawn = base * np.exp(spread * noise) if base else spread * noise
        out[name] = jnp.asarray(drawn.astype(out[name].dtype))
    for name, factor in factors.items():
        out[name] = (out[name] * factor).astype(out[name].dtype)
    return out
```

```python
import concourse.bass as bass
from concourse import mybir
from concourse.alu_op_type import AluOpType as ALU
from contextlib import ExitStack

F32 = mybir.dt.float32
BF16 = mybir.dt.bfloat16
I32 = mybir.dt.int32
U32 = mybir.dt.uint32
ACT = mybir.ActivationFunctionType
X_AXIS = mybir.AxisListType.X

B, T, D, M = 32, 112, 256, 375
DH = D // 128
KT = 3
KP = M // KT
H, HD = 16, 16
SCALE0 = HD ** -0.5
HPT = 128 // HD
E = 8
CAP = int(B * T * 2 * 1.25 / E)
FF = 512
LN_EPS = 1e-5
PAIRS = [(0, 0), (0, 1), (0, 2), (1, 0), (1, 1), (2, 0)]
STACK = len(PAIRS) * HD
NST = STACK + 3


class Chain:

    def __init__(self, eng, sem):
        self.eng, self.sem, self.n = eng, sem, 0

    def restart(self):
        self.eng.sem_clear(self.sem)
        self.n = 0

    def done(self, ins):
        ins.then_inc(self.sem, 1)
        self.n += 1
        self.eng.wait_ge(self.sem, self.n)


def hold(eng, sem, value, passed):
    eng.wait_ge(sem, value)
    eng.sem_inc(passed, 1)


class Tile:

    def __init__(self, rounds, place, period):
        self.rounds, self.place, self.period = rounds, place, period
        self.b = rounds * period + place

    def slot(self, n):
        return self.place % n

    def round(self, n):
        return self.rounds * (self.period // n) + self.place // n


def pipeline(eng, count, lags, peel, step, period=2):
    def tiles(n):
        return [Tile((n - lag) // period, (n - lag) % period, period) if 0 <= n - lag < count else None for lag in lags]
    for n in range(peel):
        step(*tiles(n))
    with eng.Fori(peel // period, count // period) as i:
        for n in range(period):
            step(*[Tile(i + (n - lag) // period, (n - lag) % period, period) for lag in lags])
    for n in range(count, count + max(lags)):
        step(*tiles(n))


def free(eng, sem, value):
    if not (isinstance(value, int) and value <= 0):
        eng.wait_ge(sem, value)


def at(ap, index):
    return ap[bass.ds(index, 1), :, :].rearrange("a p d -> p (a d)")


def at_rest(nc, signals):
    numbers = sorted(s.num for s in signals)
    first = [n for n in numbers if n - 1 not in numbers]
    last = [n for n in numbers if n + 1 not in numbers]
    with nc.Block() as block:
        @block.sync
        def _(sp):
            for lo, hi in zip(first, last):
                sp.sem_clear(range(lo, hi + 1))


def attend(nc, x, ctxT, wq, wk, wv, wp, bp, wg, gates, consts, x1_d, disp_d, slot_d, gate_d, kstage_d, qstage_d, mstage_d):
    ctx, work = ExitStack(), ExitStack()
    with ctx:
        def sb(name, shape, dt=F32):
            return ctx.enter_context(nc.sbuf_tensor(name, shape, dt))

        def sem(name):
            signals.append(ctx.enter_context(nc.semaphore(name)))
            return signals[-1]

        signals = []

        wq_s = sb("wq_s", [128, DH, D])
        wk_s = sb("wk_s", [128, DH, D])
        wv_s = sb("wv_s", [128, DH, D])
        wp_s = sb("wp_s", [128, DH, D])
        wg_s = sb("wg_s", [128, DH, E])
        cst = sb("cst", [128, 512])
        ident, before, ones, iota = cst[:, 0:128], cst[:, 128:128 + T], cst[:, 240:240 + T], cst[:, 352:480]
        gain = sb("gain", [T, 4])
        tg = sb("tg", [T, 4])
        bias = sb("bias", [T, D])
        eps = sb("eps", [T, 1])
        zeros = sb("zeros", [T, 2560])
        ct = sb("ct", [128, 2, DH, M])
        xt = sb("xt", [T, 2, D])
        stats = sb("stats", [T, 2, 6])
        mv = sb("mv", [T, 2, 2])
        lnv = sb("lnv", [T, 2])
        rstd = sb("rstd", [T, 2])
        xn = sb("xn", [T, 2, D])
        xnT = sb("xnT", [128, 2, DH, T])
        kpart = sb("kpart", [128, 2, 3, DH, M], BF16)
        krest = sb("krest", [128, 2, DH, M])
        qpart = sb("qpart", [128, 2, 3, DH, T], BF16)
        qrest = sb("qrest", [128, 2, DH, T])
        vt = sb("vt", [KP, 2, KT, H, HD + 1])
        kst = sb("kst", [NST, 2, H, M], BF16)
        qst = sb("qst", [NST, 2, H, T], BF16)
        mx = sb("mx", [T, 2, H])
        mrest = sb("mrest", [H, 2, T])
        mpart = sb("mpart", [H, 2, 3, T], BF16)
        probs = sb("probs", [KP, 2, KT, H * T])
        den = sb("den", [T, H])
        o = sb("o", [T, H, HD])
        oT = sb("oT", [128, DH, T])
        xr = sb("xr", [T, 2, D])
        x1 = sb("x1", [T, 2, D])
        st2 = sb("st2", [T, 6])
        mv2 = sb("mv2", [T, 2])
        lnv2 = sb("lnv2", [T, 1])
        rstd2 = sb("rstd2", [T, 1])
        xn2 = sb("xn2", [T, 2, D])
        xn2T = sb("xn2T", [128, DH, T])
        lg = sb("lg", [T, E])
        top = sb("top", [T, 8])
        topi = sb("topi", [T, 8], U32)
        topf = sb("topf", [T, 8])
        hot = sb("hot", [T, 2, E])
        cnt = sb("cnt", [T, E])
        total = sb("total", [T, E])
        pos = sb("pos", [T, 2, E])
        pos2 = sb("pos2", [T, 2])
        slotf = sb("slotf", [T, 2])
        over = sb("over", [T, 2])
        sent = sb("sent", [T, 2, 2], I32)
        fetch = sb("fetch", [T, 2, 2], I32)
        gx = sb("gx", [T, 2])
        gt = sb("gt", [T, 2, 2])

        bank = [ctx.enter_context(nc.psum_tensor(f"bank{i}", [128, 512], F32)) for i in range(8)]
        pT, pQ = bank[0][:, 0:DH * T], bank[0][:, DH * T:2 * DH * T]
        pKV, pS, pE, pO = bank[1:3], bank[3:5], bank[5:7], bank[7]

        weights_in, setup, vset, aset, zeroed = sem("weights_in"), sem("setup"), sem("vset"), sem("aset"), sem("zeroed")
        ct_in = [sem(f"ct_in{s}") for s in range(2)]
        x_in = [sem(f"x_in{s}") for s in range(2)]
        xr_in = [sem(f"xr_in{s}") for s in range(2)]
        kout = [sem(f"kout{s}") for s in range(2)]
        qout = [sem(f"qout{s}") for s in range(2)]
        kst_in = [sem(f"kst_in{s}") for s in range(2)]
        xr_done = sem("xr_done")
        mout = [sem(f"mout{s}") for s in range(2)]
        mst_in = [sem(f"mst_in{s}") for s in range(2)]
        x1_out = [sem(f"x1_out{s}") for s in range(2)]
        meta_out = [sem(f"meta_out{s}") for s in range(2)]
        scat = [sem(f"scat{s}") for s in range(2)]
        stat_a, rstd_a, xn_a = sem("stat_a"), sem("rstd_a"), sem("xn_a")
        xt_ps, xnT_a, q_ps, q_hi, q_rest, q_done = (sem(n) for n in ("xt_ps", "xnT_a", "q_ps", "q_hi", "q_rest", "q_done"))
        k_ps, k_hi, k_rest, k_done = (sem(n) for n in ("k_ps", "k_hi", "k_rest", "k_done"))
        v_ps, v_done = sem("v_ps"), sem("v_done")
        s_ps, s_max, max_ps, m_done = sem("s_ps"), sem("s_max"), sem("max_ps"), sem("m_done")
        e_ps, e_done = sem("e_ps"), sem("e_done")
        o_ps, o_done, oT_ps, oT_done, y_ps, x1_done = (sem(n) for n in ("o_ps", "o_done", "oT_ps", "oT_done", "y_ps", "x1_done"))
        stat_d, rstd_d, xn_d, x2T_ps, x2T_done = (sem(n) for n in ("stat_d", "rstd_d", "xn_d", "x2T_ps", "x2T_done"))
        lg_ps, lg_done, cnt_done, pos_ps, pos_done, gx_in, ex_done, meta_done, tot_done = (
            sem(n) for n in ("lg_ps", "lg_done", "cnt_done", "pos_ps", "pos_done", "gx_in", "ex_done", "meta_done", "tot_done"))
        vchain, achain, gchain = sem("vchain"), sem("achain"), sem("gchain")
        spass, gpass = sem("spass"), sem("gpass")
        block = work.enter_context(nc.Block())

        @block.sync
        def _(sp):
            for dst, src in ((wq_s, wq), (wk_s, wk), (wv_s, wv), (wp_s, wp), (wg_s, wg)):
                sp.dma_start(dst[:, :, :], src.rearrange("(h p) n -> p h n", p=128)).then_inc(weights_in, 16)
            sp.dma_start(cst[:, :], consts).then_inc(weights_in, 16)
            sp.dma_start(gain[:, :], gates).then_inc(weights_in, 16)
            sp.dma_start(bias[:, :], bp).then_inc(weights_in, 16)

            def need(signal, value):
                if not (isinstance(value, int) and value <= 0):
                    hold(sp, signal, value, spass)

            def step(load, proj, score, done):
                if load:
                    b, s, r = load.b, load.slot(2), load.round(2)
                    need(v_ps, (b - 1) * 2)
                    need(xn_a, b - 1)
                    sp.dma_start(ct[:, s, :, :], ctxT[bass.ds(b, 1), :, :].rearrange("a (h p) m -> p (a h) m", p=128)).then_inc(ct_in[s], 16)
                    sp.dma_start(xt[:, s, :], at(x, b)).then_inc(x_in[s], 16)
                if done:
                    b, s, r = done.b, done.slot(2), done.round(2)
                    need(x1_done, b - 1)
                    sp.dma_start(xr[:, s, :], at(x, b)).then_inc(xr_in[s], 16)
                if proj:
                    b, s, r = proj.b, proj.slot(2), proj.round(2)
                    need(q_done, b + 1)
                    need(kst_in[s], r * 192)
                    sp.dma_start(qstage_d[s].rearrange("(n p) f -> p n f", p=128), qpart[:, s].rearrange("p a h m -> p (a h) m")).then_inc(qout[s], 16)
                    need(k_done, b + 1)
                    sp.dma_start(kstage_d[s].rearrange("(n p) f -> p n f", p=128), kpart[:, s].rearrange("p a h m -> p (a h) m")).then_inc(kout[s], 16)
                    need(e_ps, (b - 1) * 12)
                    kv = kstage_d[s].rearrange("(a h d) f -> a d h f", d=HD, a=3)
                    qv = qstage_d[s].rearrange("(a h d) f -> a d h f", d=HD, a=3)
                    need(qout[s], 16 * (r + 1))
                    need(kout[s], 16 * (r + 1))
                    for n, (qp, kp) in enumerate(PAIRS):
                        rows = slice(n * HD, (n + 1) * HD)
                        sp.dma_start(kst[rows, s, :, :], kv[kp]).then_inc(kst_in[s], 16)
                        sp.dma_start(qst[rows, s, :, :], qv[qp]).then_inc(kst_in[s], 16)
                if score:
                    b, s, r = score.b, score.slot(2), score.round(2)
                    need(m_done, b + 1)
                    need(mst_in[s], 16 * r)
                    sp.dma_start(mstage_d[s], mpart[:, s].rearrange("h a t -> h (a t)")).then_inc(mout[s], 16)
                    need(mout[s], 16 * (r + 1))
                    sp.dma_start(qst[STACK:NST, s, :, :], mstage_d[s].rearrange("h (a t) -> a h t", a=3)).then_inc(mst_in[s], 16)
                if done:
                    b, s, r = done.b, done.slot(2), done.round(2)
                    need(x1_done, b + 1)
                    sp.dma_start(at(x1_d, b), x1[:, s, :]).then_inc(x1_out[s], 16)
                    need(meta_done, b + 1)
                    sp.dma_start(at(slot_d, b), fetch[:, s, :]).then_inc(meta_out[s], 16)
                    sp.dma_start(at(gate_d, b), gt[:, s, :]).then_inc(meta_out[s], 16)

            pipeline(sp, B, (0, 1, 2, 3), 6, step)
            for s in range(2):
                sp.wait_ge(x1_out[s], 16 * (B // 2))
                sp.wait_ge(meta_out[s], 32 * (B // 2))

        @block.gpsimd
        def _(pool):
            chain = Chain(pool, gchain)
            chain.done(pool.memset(eps[:, :], LN_EPS))
            chain.done(pool.memset(zeros[:, :], 0.0))
            chain.done(pool.memset(kst[96:NST, :, :, :], 1.0))
            chain.done(pool.memset(vt[:, :, :, :, HD:HD + 1], 1.0))
            chain.done(pool.memset(total[:, :], 0.0))
            pool.sem_inc(setup, 1)
            every = disp_d.rearrange("(p n a) d -> n p (a d)", p=T, n=8)
            for n in range(8):
                pool.dma_start(every[n], zeros[:, :]).then_inc(zeroed, 16)
            pool.wait_ge(zeroed, 128)

            def split(b, s, part, rest, taken, given):
                hold(pool, taken, b, gpass)
                chain.restart()
                chain.done(pool.tensor_copy(part[:, s, 1], rest[:, s]))
                pool.tensor_tensor(part[:, s, 2], rest[:, s], part[:, s, 1], ALU.subtract).then_inc(given, 1)

            def step(proj, score, done):
                if done:
                    b, s, r = done.b, done.slot(2), done.round(2)
                    hold(pool, xr_in[s], 16 * (r + 1), gpass)
                    pool.tensor_tensor(xr[:, s, :], xr[:, s, :], bias[:, :], ALU.add).then_inc(xr_done, 1)
                if proj:
                    b, s, r = proj.b, proj.slot(2), proj.round(2)
                    split(b + 1, s, qpart, qrest, q_rest, q_done)
                    split((b + 1) * 2, s, kpart, krest, k_rest, k_done)
                if done:
                    hold(pool, meta_done, done.b + 1, gpass)
                    b, s, r = done.b, done.slot(2), done.round(2)
                    for k in range(2):
                        pool.indirect_dma_start(disp_d, bass.IndirectOffsetOnAxis(ap=sent[:, s, k:k + 1], axis=0),
                                                xn2[:, s, :], None, bounds_check=E * CAP - 1, oob_is_err=False).then_inc(scat[s], 16)

            pool.wait_ge(vset, 1)
            pipeline(pool, B, (0, 1, 2), 4, step)
            for s in range(2):
                pool.wait_ge(scat[s], 32 * (B // 2))

        @block.scalar
        def _(act):
            chain = Chain(act, achain)
            act.wait_ge(weights_in, 128)
            act.wait_ge(setup, 1)
            act.activation(tg[:, :], gain[:, :], ACT.Tanh).then_inc(aset, 1)
            act.preload_act_table_set("natural_log_exp_and_others")

            def inverse_root(taken, value, var, log, out, given):
                chain.restart()
                act.wait_ge(taken, value)
                chain.done(act.activation(log, var, ACT.Ln, bias=eps[:, 0:1]))
                act.activation(out, log, ACT.Exp, scale=-0.5).then_inc(given, 1)

            def step(proj, score, done):
                def exps(first, last):
                    if score:
                        b, s, r = score.b, score.slot(2), score.round(2)
                        for u in range(first, last):
                            act.wait_ge(e_ps, b * 12 + u + 1)
                            if u == 0:
                                free(act, o_ps, b - 1)
                            t, g = u // 4, u % 4
                            act.activation(probs[:, s, t, g * 4 * T:(g + 1) * 4 * T], pE[u % 2][0:KP, 0:4 * T], ACT.Exp,
                                           scale=SCALE0).then_inc(e_done, 1)
                if proj:
                    b, s, r = proj.b, proj.slot(2), proj.round(2)
                    inverse_root(stat_a, b + 1, mv[:, s, 1:2], lnv[:, s:s + 1], rstd[:, s:s + 1], rstd_a)
                    act.wait_ge(q_ps, b + 1)
                    free(act, qout[s], 16 * r)
                    act.copy(qpart[:, s, 0].rearrange("p h t -> p (h t)"), pQ).then_inc(q_hi, 1)
                    for m in range(DH):
                        act.wait_ge(k_ps, b * 2 + m + 1)
                        free(act, kout[s], 16 * r)
                        act.copy(kpart[:, s, 0, m], pKV[m][:, 0:M]).then_inc(k_hi, 1)
                    for n, (lo, hi) in enumerate(((0, 2), (2, 3))):
                        act.wait_ge(v_ps, b * 2 + n + 1)
                        free(act, o_ps, b - 1)
                        act.copy(vt[:, s, lo:hi, :, 0:HD],
                                 pKV[n][0:KP, 0:(hi - lo) * D].rearrange("p (t h d) -> p t h d", t=hi - lo, h=H)).then_inc(v_done, 1)
                exps(0, 2)
                if done:
                    b, s, r = done.b, done.slot(2), done.round(2)
                    act.wait_ge(oT_ps, b + 1)
                    act.copy(oT[:, :, :].rearrange("p h t -> p (h t)"), pO[:, 0:DH * T]).then_inc(oT_done, 1)
                exps(2, 4)
                if done:
                    inverse_root(stat_d, b + 1, mv2[:, 1:2], lnv2[:, :], rstd2[:, :], rstd_d)
                exps(4, 7)
                if done:
                    b, s, r = done.b, done.slot(2), done.round(2)
                    act.wait_ge(x2T_ps, b + 1)
                    act.copy(xn2T[:, :, :].rearrange("p h t -> p (h t)"), pO[:, 0:DH * T]).then_inc(x2T_done, 1)
                exps(7, 9)
                if done:
                    b, s, r = done.b, done.slot(2), done.round(2)
                    act.wait_ge(gx_in, b + 1)
                    act.activation(gx[:, 1:2], gx[:, 0:1], ACT.Exp).then_inc(ex_done, 1)
                exps(9, 12)

            pipeline(act, B, (0, 1, 2), 4, step)

        @block.vector
        def _(v):
            chain = Chain(v, vchain)
            v.wait_ge(aset, 1)
            chain.done(v.tensor_scalar(bias[:, :], bias[:, :], tg[:, 0:1], None, ALU.mult))
            v.sem_inc(vset, 1)

            def moments(x_in_sem, value, rows, st, out, given):
                chain.restart()
                v.wait_ge(x_in_sem, value)
                chain.done(v.bn_stats(st, rows))
                v.bn_aggr(out, st).then_inc(given, 1)

            def step(proj, score, done):
                def maxima(first, last):
                    if score:
                        b, s, r = score.b, score.slot(2), score.round(2)
                        for h in range(first, last):
                            v.wait_ge(s_ps, b * H + h + 1)
                            v.reduce_max(mx[:, s, h:h + 1], pS[h % 2][0:T, 0:M], axis=X_AXIS).then_inc(s_max, 1)

                if proj:
                    b, s, r = proj.b, proj.slot(2), proj.round(2)
                    moments(x_in[s], 16 * (r + 1), xt[:, s, :], stats[:, s], mv[:, s], stat_a)
                maxima(0, 2)
                if proj:
                    v.wait_ge(rstd_a, proj.b + 1)
                    v.tensor_scalar(xn[:, proj.slot(2), :], xt[:, proj.slot(2), :], mv[:, proj.slot(2), 0:1], rstd[:, proj.slot(2):proj.slot(2) + 1],
                                    ALU.subtract, ALU.mult).then_inc(xn_a, 1)
                maxima(2, 4)
                if proj:
                    b, s, r = proj.b, proj.slot(2), proj.round(2)
                    v.wait_ge(xt_ps, b + 1)
                    v.tensor_copy(xnT[:, s].rearrange("p h t -> p (h t)"), pT).then_inc(xnT_a, 1)
                maxima(4, 6)
                if proj:
                    b, s, r = proj.b, proj.slot(2), proj.round(2)
                    v.wait_ge(q_hi, b + 1)
                    free(v, q_done, b - 1)
                    v.tensor_tensor(qrest[:, s].rearrange("p h t -> p (h t)"), pQ, qpart[:, s, 0].rearrange("p h t -> p (h t)"),
                                    ALU.subtract).then_inc(q_rest, 1)
                for m in range(DH):
                    maxima(6 + 2 * m, 8 + 2 * m)
                    if proj:
                        b, s, r = proj.b, proj.slot(2), proj.round(2)
                        v.wait_ge(k_hi, b * 2 + m + 1)
                        free(v, k_done, b - 1)
                        v.tensor_tensor(krest[:, s, m], pKV[m][:, 0:M], kpart[:, s, 0, m], ALU.subtract).then_inc(k_rest, 1)
                maxima(10, 16)
                if score:
                    b, s, r = score.b, score.slot(2), score.round(2)
                    chain.restart()
                    v.wait_ge(max_ps, b + 1)
                    free(v, mout[s], 16 * r)
                    chain.done(v.tensor_scalar(mpart[:, s, 0], pS[0][0:H, 0:T], -1.0, None, ALU.mult))
                    chain.done(v.scalar_tensor_tensor(mrest[:, s], pS[0][0:H, 0:T], -1.0, mpart[:, s, 0], ALU.mult, ALU.subtract))
                    chain.done(v.tensor_copy(mpart[:, s, 1], mrest[:, s]))
                    v.tensor_tensor(mpart[:, s, 2], mrest[:, s], mpart[:, s, 1], ALU.subtract).then_inc(m_done, 1)
                if done:
                    b, s, r = done.b, done.slot(2), done.round(2)
                    pv = pO[0:T, 0:H * (HD + 1)].rearrange("p (h d) -> p h d", h=H)
                    chain.restart()
                    v.wait_ge(o_ps, b + 1)
                    chain.done(v.reciprocal(den[:, :], pv[:, :, HD]))
                    v.tensor_tensor(o[:, :, :], pv[:, :, 0:HD], den[:, :].unsqueeze(2).broadcast_to((T, H, HD)), ALU.mult).then_inc(o_done, 1)
                    v.wait_ge(y_ps, b + 1)
                    v.wait_ge(xr_done, b + 1)
                    free(v, x1_out[s], 16 * r)
                    v.scalar_tensor_tensor(x1[:, s, :], pO[0:T, 0:D], tg[:, 0:1], xr[:, s, :], ALU.mult, ALU.add).then_inc(x1_done, 1)
                    moments(x1_done, b + 1, x1[:, s, :], st2[:, :], mv2[:, :], stat_d)
                    v.wait_ge(rstd_d, b + 1)
                    free(v, scat[s], 32 * r)
                    v.tensor_scalar(xn2[:, s, :], x1[:, s, :], mv2[:, 0:1], rstd2[:, :], ALU.subtract, ALU.mult).then_inc(xn_d, 1)
                    chain.restart()
                    v.wait_ge(lg_ps, b + 1)
                    chain.done(v.tensor_copy(lg[:, :], pO[0:T, 0:E]))
                    chain.done(v.max(top[:, :], lg[:, :]))
                    chain.done(v.max_index(topi[:, :], top[:, :], lg[:, :]))
                    chain.done(v.tensor_copy(topf[:, 0:2], topi[:, 0:2]))
                    for k in range(2):
                        chain.done(v.tensor_scalar(hot[:, k, :], iota[0:T, 0:E], topf[:, k:k + 1], None, ALU.is_equal))
                    v.tensor_tensor(cnt[:, :], hot[:, 0, :], hot[:, 1, :], ALU.add).then_inc(cnt_done, 1)
                    v.tensor_tensor(gx[:, 0:1], top[:, 1:2], top[:, 0:1], ALU.subtract).then_inc(gx_in, 1)
                    v.wait_ge(pos_ps, b + 1)
                    v.tensor_tensor(pos[:, :, :], hot[:, :, :], pO[0:T, 0:E].unsqueeze(1).broadcast_to((T, 2, E)), ALU.mult).then_inc(pos_done, 1)
                    v.wait_ge(pos_done, b + 1)
                    chain.done(v.reduce_sum(pos2[:, :], pos[:, :, :], axis=X_AXIS))
                    chain.done(v.tensor_scalar(over[:, :], pos2[:, :], float(CAP), None, ALU.is_ge))
                    chain.done(v.tensor_scalar(pos2[:, :], pos2[:, :], float(CAP - 1), None, ALU.min))
                    chain.done(v.scalar_tensor_tensor(slotf[:, :], topf[:, 0:2], float(CAP), pos2[:, :], ALU.mult, ALU.add))
                    free(v, meta_out[s], 32 * r)
                    chain.done(v.tensor_copy(fetch[:, s, :], slotf[:, :]))
                    chain.done(v.scalar_tensor_tensor(slotf[:, :], over[:, :], float(1 << 20), slotf[:, :], ALU.mult, ALU.add))
                    chain.done(v.tensor_copy(sent[:, s, :], slotf[:, :]))
                    chain.done(v.tensor_tensor(total[:, :], total[:, :], cnt[:, :], ALU.add))
                    v.wait_ge(ex_done, b + 1)
                    chain.done(v.tensor_scalar(gx[:, 0:1], gx[:, 1:2], 1.0, None, ALU.add))
                    chain.done(v.reciprocal(gt[:, s, 0:1], gx[:, 0:1]))
                    chain.done(v.tensor_tensor(gt[:, s, 1:2], gt[:, s, 0:1], gx[:, 1:2], ALU.mult))
                    chain.done(v.tensor_scalar(over[:, :], over[:, :], -1.0, 1.0, ALU.mult, ALU.add))
                    v.tensor_tensor(gt[:, s, :], gt[:, s, :], over[:, :], ALU.mult).then_inc(meta_done, 1)

            pipeline(v, B, (0, 1, 2), 4, step)

        @block.tensor
        def _(pe):
            pe.wait_ge(weights_in, 128)
            pe.wait_ge(setup, 1)

            def step(proj, score, done):
                def scores(first, last):
                    if score:
                        b, s, r = score.b, score.slot(2), score.round(2)
                        for h in range(first, last):
                            if h == 0:
                                pe.wait_ge(kst_in[s], 192 * (r + 1))
                                free(pe, m_done, b)
                            free(pe, s_max, b * H + h - 1)
                            pe.matmul(pS[h % 2][0:T, 0:M], qst[0:STACK, s, h, :], kst[0:STACK, s, h, :], start=True, stop=True).then_inc(s_ps, 1)

                def transposed(first, last):
                    if score:
                        b, s, r = score.b, score.slot(2), score.round(2)
                        for u in range(first, last):
                            if u == 0:
                                pe.wait_ge(mst_in[s], 16 * (r + 1))
                            t, g = u // 4, u % 4
                            free(pe, e_done, b * 12 + u - 1)
                            for h in range(4):
                                last_mm = pe.matmul(pE[u % 2][0:KP, h * T:(h + 1) * T], kst[:, s, g * 4 + h, t * KP:(t + 1) * KP],
                                                    qst[:, s, g * 4 + h, :], start=True, stop=True)
                            last_mm.then_inc(e_ps, 1)

                scores(0, 2)
                if proj:
                    b, s, r = proj.b, proj.slot(2), proj.round(2)
                    pe.wait_ge(xn_a, b + 1)
                    free(pe, q_rest, b)
                    for h in range(DH):
                        mm = pe.transpose(pT[:, h * T:(h + 1) * T], xn[:, s, h * 128:(h + 1) * 128], ident[0:T, 0:T])
                    mm.then_inc(xt_ps, 1)
                scores(2, 4)
                if proj:
                    b, s, r = proj.b, proj.slot(2), proj.round(2)
                    pe.wait_ge(xnT_a, b + 1)
                    for m in range(DH):
                        for h in range(DH):
                            mm = pe.matmul(pQ[:, m * T:(m + 1) * T], wq_s[:, h, m * 128:(m + 1) * 128], xnT[:, s, h, :],
                                           start=h == 0, stop=h == DH - 1)
                    mm.then_inc(q_ps, 1)
                for m in range(DH):
                    scores(4 + 2 * m, 6 + 2 * m)
                    if proj:
                        b, s, r = proj.b, proj.slot(2), proj.round(2)
                        if m == 0:
                            pe.wait_ge(ct_in[s], 16 * (r + 1))
                            free(pe, v_done, b * 2)
                        for h in range(DH):
                            mm = pe.matmul(pKV[m][:, 0:M], wk_s[:, h, m * 128:(m + 1) * 128], ct[:, s, h, :],
                                           start=h == 0, stop=h == DH - 1)
                        mm.then_inc(k_ps, 1)
                scores(8, 12)
                for n in range(2):
                    if proj:
                        b, s, r = proj.b, proj.slot(2), proj.round(2)
                        pe.wait_ge(k_rest, b * 2 + n + 1)
                        for t in ((0, 1), (2,))[n]:
                            for h in range(DH):
                                mm = pe.matmul(pKV[n][0:KP, (t % 2) * D:(t % 2 + 1) * D], ct[:, s, h, t * KP:(t + 1) * KP], wv_s[:, h, :],
                                               start=h == 0, stop=h == DH - 1)
                        mm.then_inc(v_ps, 1)
                    scores(12 + 2 * n, 14 + 2 * n)
                if score:
                    b, s, r = score.b, score.slot(2), score.round(2)
                    pe.wait_ge(s_max, (b + 1) * H)
                    pe.transpose(pS[0][0:H, 0:T], mx[:, s, :], ident[0:T, 0:T]).then_inc(max_ps, 1)
                if done:
                    b, s, r = done.b, done.slot(2), done.round(2)
                    pe.wait_ge(e_done, (b + 1) * 12)
                    pe.wait_ge(v_done, (b + 1) * 2)
                    free(pe, pos_done, b)
                    for h in range(H):
                        for t in range(KT):
                            mm = pe.matmul(pO[0:T, h * (HD + 1):(h + 1) * (HD + 1)], probs[:, s, t, h * T:(h + 1) * T], vt[:, s, t, h, :],
                                           start=t == 0, stop=t == KT - 1)
                    mm.then_inc(o_ps, 1)
                transposed(0, 2)
                if done:
                    pe.wait_ge(o_done, done.b + 1)
                    for h in range(DH):
                        mm = pe.transpose(pO[:, h * T:(h + 1) * T], o[:, h * HPT:(h + 1) * HPT, :].rearrange("p h d -> p (h d)"), ident[0:T, 0:T])
                    mm.then_inc(oT_ps, 1)
                transposed(2, 4)
                if done:
                    pe.wait_ge(oT_done, done.b + 1)
                    for h in range(DH):
                        mm = pe.matmul(pO[0:T, 0:D], oT[:, h, :], wp_s[:, h, :], start=h == 0, stop=h == DH - 1)
                    mm.then_inc(y_ps, 1)
                transposed(4, 7)
                if done:
                    b, s, r = done.b, done.slot(2), done.round(2)
                    pe.wait_ge(xn_d, b + 1)
                    for h in range(DH):
                        mm = pe.transpose(pO[:, h * T:(h + 1) * T], xn2[:, s, h * 128:(h + 1) * 128], ident[0:T, 0:T])
                    mm.then_inc(x2T_ps, 1)
                transposed(7, 9)
                if done:
                    b, s, r = done.b, done.slot(2), done.round(2)
                    pe.wait_ge(x2T_done, b + 1)
                    for h in range(DH):
                        mm = pe.matmul(pO[0:T, 0:E], xn2T[:, h, :], wg_s[:, h, :], start=h == 0, stop=h == DH - 1)
                    mm.then_inc(lg_ps, 1)
                transposed(9, 12)
                if done:
                    b, s, r = done.b, done.slot(2), done.round(2)
                    pe.wait_ge(cnt_done, b + 1)
                    pe.wait_ge(gx_in, b + 1)
                    free(pe, meta_done, b)
                    pe.matmul(pO[0:T, 0:E], before[0:T, :], cnt[:, :], start=True, stop=False)
                    pe.matmul(pO[0:T, 0:E], ones[0:T, :], total[:, :], start=False, stop=True).then_inc(pos_ps, 1)

            pipeline(pe, B, (0, 1, 2), 4, step)

        work.close()
        at_rest(nc, signals)




CH = 224
UNITS = E * CAP // CH
PER = CAP // CH
RT = CH // T
FT = FF // 128


def experts(nc, w1, w2, consts, disp_d, eout_d):
    ctx, work = ExitStack(), ExitStack()
    with ctx:
        def sb(name, shape, dt=F32):
            return ctx.enter_context(nc.sbuf_tensor(name, shape, dt))

        def sem(name):
            signals.append(ctx.enter_context(nc.semaphore(name)))
            return signals[-1]

        signals = []

        ident = sb("ident_b", [128, 128])
        w1_s = sb("w1_s", [128, 2, DH, 2 * FF])
        w2_s = sb("w2_s", [128, 2, FT, D])
        rows = sb("rows", [T, 2, RT, D])
        rowsT = sb("rowsT", [128, 2, DH, CH])
        act_g = sb("act_g", [128, 2, CH])
        hT = sb("hT", [128, 2, FT, CH])
        y = sb("y", [T, 2, RT, D])
        bank = [ctx.enter_context(nc.psum_tensor(f"ebank{i}", [128, 512], F32)) for i in range(8)]
        pT, pH, pY = bank[0:2], bank[2:6], bank[6:8]

        id_in, spass, gpass = sem("id_in"), sem("spass_b"), sem("gpass_b")
        w_in = [sem(f"w_in{s}") for s in range(2)]
        rows_in = [sem(f"rows_in{s}") for s in range(2)]
        y_out = [sem(f"y_out{s}") for s in range(2)]
        t_ps, t_done, h_ps, g_done, h_done, y_ps, y_done = (
            sem(n) for n in ("t_ps", "t_done", "h_ps", "g_done", "h_done", "y_ps_b", "y_done"))
        block = work.enter_context(nc.Block())
        disp_v = disp_d.rearrange("(u t p) d -> u p t d", t=RT, p=T)
        eout_v = eout_d.rearrange("(u t p) d -> u p t d", t=RT, p=T)

        def unit(ap, b):
            return ap[bass.ds(b, 1)].rearrange("a p t d -> p (a t) d")

        @block.sync
        def _(sp):
            def need(signal, value):
                if not (isinstance(value, int) and value <= 0):
                    hold(sp, signal, value, spass)

            sp.dma_start(ident[:, :], consts[:, 0:128]).then_inc(id_in, 16)

            def step(tile):
                b, s = tile.b, tile.slot(2)
                if tile.place % PER == 0:
                    ws = tile.slot(2 * PER) // PER
                    expert = tile.rounds * 2 + ws
                    need(y_ps, b - PER)
                    sp.dma_start(w1_s[:, ws], w1[bass.ds(expert, 1), :, :].rearrange("a (h p) n -> p (a h) n", p=128)).then_inc(w_in[ws], 16)
                    sp.dma_start(w2_s[:, ws], w2[bass.ds(expert, 1), :, :].rearrange("a (h p) n -> p (a h) n", p=128)).then_inc(w_in[ws], 16)
                need(t_ps, b - 1)
                sp.dma_start(rows[:, s], unit(disp_v, b)).then_inc(rows_in[s], 16)

            pipeline(sp, UNITS, (0,), 2 * PER, step, 2 * PER)

        @block.gpsimd
        def _(pool):
            def step(tile):
                hold(pool, y_done, tile.b + 1, gpass)
                s = tile.slot(2)
                pool.dma_start(unit(eout_v, tile.b), y[:, s]).then_inc(y_out[s], 16)

            pipeline(pool, UNITS, (0,), 2 * PER, step, 2 * PER)
            for s in range(2):
                pool.wait_ge(y_out[s], 16 * (UNITS // 2))

        @block.scalar
        def _(act):
            act.preload_act_table(ACT.Gelu)

            def step(up):
                if up:
                    for j in range(FT):
                        act.wait_ge(h_ps, up.b * FT + j + 1)
                        free(act, h_done, up.b * FT + j - 1)
                        act.activation(act_g[:, j % 2, :], pH[j][:, 0:CH], ACT.Gelu).then_inc(g_done, 1)

            pipeline(act, UNITS, (0,), 2 * PER, step, 2 * PER)

        @block.vector
        def _(v):
            def step(turn, up, down):
                if turn:
                    s = turn.slot(2)
                    v.wait_ge(t_ps, turn.b + 1)
                    free(v, h_ps, (turn.b - 1) * FT)
                    v.tensor_copy(rowsT[:, s].rearrange("p h c -> p (h c)"), pT[s][:, 0:DH * CH]).then_inc(t_done, 1)
                if down:
                    s = down.slot(2)
                    v.wait_ge(y_ps, down.b + 1)
                    free(v, y_out[s], 16 * down.round(2))
                    v.tensor_copy(y[:, s].rearrange("p t d -> p (t d)"), pY[s][0:T, :]).then_inc(y_done, 1)
                if up:
                    s = up.slot(2)
                    for j in range(FT):
                        v.wait_ge(g_done, up.b * FT + j + 1)
                        free(v, y_ps, up.b - 1)
                        v.tensor_tensor(hT[:, s, j, :], act_g[:, j % 2, :], pH[j][:, CH:2 * CH], ALU.mult).then_inc(h_done, 1)

            pipeline(v, UNITS, (0, 1, 2), 2 * PER, step, 2 * PER)

        @block.tensor
        def _(pe):
            pe.wait_ge(id_in, 16)

            def step(turn, up, down):
                if turn:
                    s = turn.slot(2)
                    pe.wait_ge(rows_in[s], 16 * (turn.round(2) + 1))
                    free(pe, t_done, turn.b - 1)
                    for h in range(DH):
                        for t in range(RT):
                            mm = pe.transpose(pT[s][:, h * CH + t * T:h * CH + (t + 1) * T], rows[:, s, t, h * 128:(h + 1) * 128], ident[0:T, 0:T])
                    mm.then_inc(t_ps, 1)
                if down:
                    s, ws = down.slot(2), down.place // PER
                    pe.wait_ge(h_done, (down.b + 1) * FT)
                    free(pe, y_done, down.b - 1)
                    for t in range(RT):
                        for j in range(FT):
                            mm = pe.matmul(pY[s][0:T, t * D:(t + 1) * D], hT[:, s, j, t * T:(t + 1) * T], w2_s[:, ws, j, :],
                                           start=j == 0, stop=j == FT - 1)
                    mm.then_inc(y_ps, 1)
                if up:
                    s, ws = up.slot(2), up.place // PER
                    if up.place % PER == 0:
                        pe.wait_ge(w_in[ws], 32 * (up.rounds + 1))
                    pe.wait_ge(t_done, up.b + 1)
                    for j in range(FT):
                        free(pe, h_done, (up.b - 1) * FT + j + 1)
                        for g in range(2):
                            for h in range(DH):
                                col = (g * FT + j) * 128
                                mm = pe.matmul(pH[j][:, g * CH:(g + 1) * CH], w1_s[:, ws, h, col:col + 128], rowsT[:, s, h, :],
                                               start=h == 0, stop=h == DH - 1)
                        mm.then_inc(h_ps, 1)

            pipeline(pe, UNITS, (0, 1, 2), 2 * PER, step, 2 * PER)

        work.close()
        at_rest(nc, signals)




SCALE1 = D ** -0.5


def cross(nc, x1_d, eout_d, slot_d, gate_d, ctxT, ctxN, wqc, wks, wkc, wqs, wvsT, wvcT, wgT, bcols, brows, gates, consts, interp, x2_d, x3_d):
    ctx, work = ExitStack(), ExitStack()
    with ctx:
        def sb(name, shape, dt=F32):
            return ctx.enter_context(nc.sbuf_tensor(name, shape, dt))

        def sem(name):
            signals.append(ctx.enter_context(nc.semaphore(name)))
            return signals[-1]

        signals = []

        cst = sb("cst_c", [128, 512])
        ident = cst[:, 0:128]
        onerow = sb("onerow", [1, 128])
        wraw = sb("wraw", [128, 4, DH, D])
        wvs, wvc = sb("wvs", [128, DH, D]), sb("wvc", [128, DH, D])
        wg = sb("wg_c", [128, 2 * DH, D])
        bc = sb("bc", [128, DH, 4])
        br = sb("br", [T, 3, D])
        gain, tg, eps = sb("gain_c", [T, 4]), sb("tg_c", [T, 4]), sb("eps_c", [T, 1])
        win = sb("win", [KP, KT, T])
        g1, g2 = sb("g1", [128, DH, D]), sb("g2", [128, DH, D])
        g1b, g2b, w2 = sb("g1b", [128, DH]), sb("g2b", [128, DH]), sb("w2", [128, DH])
        bb = sb("bb", [1, 1])
        x1 = sb("x1_c", [T, 2, D])
        slots = sb("slots", [T, 2, 2], I32)
        gt = sb("gt_c", [T, 2, 2])
        wt = sb("wt", [T, 2])
        er = sb("er", [T, 2, 2, D])
        x2 = sb("x2", [T, 4, D])
        st, mv, lnv, rstd = sb("st_c", [T, 6]), sb("mv_c", [T, 2]), sb("lnv_c", [T, 1]), sb("rstd_c", [T, 1])
        xn, xnT = sb("xn_c", [T, D]), sb("xnT_c", [128, DH, T])
        aT = sb("aT", [128, 2, 2, DH, T])
        vc = sb("vc", [T, 4, D])
        dr = sb("dr", [1, 2, T])
        ct = sb("ct_c", [128, 2, DH, M])
        cn = sb("cn", [KP, 4, KT, D])
        m1, n1, l1, r1 = sb("m1", [T, 1]), sb("n1", [T, 1]), sb("l1", [T, 1]), sb("r1", [T, 2])
        m2, n2, l2, r2 = sb("m2", [KP, KT]), sb("n2", [KP, KT]), sb("l2", [KP, KT]), sb("r2", [KP, KT])
        p1, p1T = sb("p1", [T, M]), sb("p1T", [KP, 2, KT, T])
        p2, p2n = sb("p2", [KP, KT, T]), sb("p2n", [KP, 2, KT, T])
        c1T, p2iT = sb("c1T", [128, DH, T]), sb("p2iT", [T, T])
        both = sb("both", [T, 2, 2, D])
        bT = sb("bT", [128, 2 * DH, T])
        gl, ge, gr, df = sb("gl", [T, D]), sb("ge", [T, D]), sb("gr", [T, D]), sb("df", [T, D])
        x3 = sb("x3", [T, 2, D])

        bank = [ctx.enter_context(nc.psum_tensor(f"cbank{i}", [128, 512], F32)) for i in range(8)]
        bX, bA, bV, bS1, bS2, bR, bC, bG = bank

        w_in, setup, vset, spass, gpass, vpass = (sem(n) for n in ("w_in_c", "setup_c", "vset_c", "spass_c", "gpass_c", "vpass_c"))
        wset_ps = sem("wset_ps")
        x1_in = [sem(f"x1_in{s}") for s in range(2)]
        meta_in = [sem(f"meta_in{s}") for s in range(2)]
        er_in = [sem(f"er_in{s}") for s in range(2)]
        ct_in = [sem(f"ct_in_c{s}") for s in range(2)]
        cn_in = [sem(f"cn_in{s}") for s in range(4)]
        x3_out = [sem(f"x3_out{s}") for s in range(2)]
        (x2_done, stat_done, rstd_done, xn_done, xt_ps, xnT_done, a_ps, a_done, v_ps, v_done,
         s1_ps, s2_ps, n1_done, n2_done, e1_done, e2_done, t1_ps, t1_done, p2_done,
         c_ps, c_done, y_ps, y_done, gt_ps, gt_done, g_ps, gl_done, ge_done, x3_done) = (sem(n + "_c") for n in (
             "x2_done stat_done rstd_done xn_done xt_ps xnT_done a_ps a_done v_ps v_done "
             "s1_ps s2_ps n1_done n2_done e1_done e2_done t1_ps t1_done p2_done "
             "c_ps c_done y_ps y_done gt_ps gt_done g_ps gl_done ge_done x3_done").split())
        vchain, achain = sem("vchain_c"), sem("achain_c")
        block = work.enter_context(nc.Block())
        PERIOD, PEEL = 4, 8

        @block.sync
        def _(sp):
            def need(signal, value):
                if not (isinstance(value, int) and value <= 0):
                    hold(sp, signal, value, spass)

            for n, w in enumerate((wqc, wks, wkc, wqs)):
                sp.dma_start(wraw[:, n], w.rearrange("(h p) n -> p h n", p=128)).then_inc(w_in, 16)
            for dst, w in ((wvs, wvsT), (wvc, wvcT), (wg, wgT), (bc, bcols)):
                sp.dma_start(dst[:, :, :], w.rearrange("(h p) n -> p h n", p=128)).then_inc(w_in, 16)
            sp.dma_start(br[:, :, :], brows).then_inc(w_in, 16)
            sp.dma_start(gain[:, :], gates).then_inc(w_in, 16)
            sp.dma_start(cst[:, :], consts).then_inc(w_in, 16)
            sp.dma_start(win[:, :, :], interp).then_inc(w_in, 16)

            def step(load, ctxs, out):
                if load:
                    b, s = load.b, load.slot(2)
                    need(er_in[s], 32 * load.round(2))
                    need(x2_done, b - 1)
                    sp.dma_start(slots[:, s, :], at(slot_d, b)).then_inc(meta_in[s], 16)
                    sp.dma_start(gt[:, s, :], at(gate_d, b)).then_inc(meta_in[s], 16)
                    sp.dma_start(x1[:, s, :], at(x1_d, b)).then_inc(x1_in[s], 16)
                if ctxs:
                    b, s = ctxs.b, ctxs.slot(2)
                    need(s2_ps, b - 1)
                    sp.dma_start(ct[:, s], ctxT[bass.ds(b, 1), :, :].rearrange("a (h p) m -> p (a h) m", p=128)).then_inc(ct_in[s], 16)
                    need(c_ps, b - 3)
                    sp.dma_start(cn[:, ctxs.slot(4)], ctxN[bass.ds(b, 1), :, :].rearrange("a (t p) d -> p (a t) d", p=KP)).then_inc(cn_in[ctxs.slot(4)], 16)
                if out:
                    b, s = out.b, out.slot(2)
                    need(x3_done, b + 1)
                    sp.dma_start(at(x3_d, b), x3[:, s, :]).then_inc(x3_out[s], 16)

            pipeline(sp, B, (0, 1, 5), PEEL, step, PERIOD)
            for s in range(2):
                sp.wait_ge(x3_out[s], 16 * (B // 2))

        @block.gpsimd
        def _(pool):
            pool.memset(eps[:, :], LN_EPS).then_inc(setup, 1)
            pool.wait_ge(setup, 1)
            pool.memset(onerow[:, :], 1.0).then_inc(setup, 1)

            def step(load):
                b, s = load.b, load.slot(2)
                hold(pool, meta_in[s], 32 * (load.round(2) + 1), gpass)
                if not (isinstance(b, int) and b < 2):
                    hold(pool, x2_done, b - 1, gpass)
                for k in range(2):
                    pool.indirect_dma_start(er[:, s, k, :], None, eout_d, bass.IndirectOffsetOnAxis(ap=slots[:, s, k:k + 1], axis=0),
                                            bounds_check=E * CAP - 1, oob_is_err=False).then_inc(er_in[s], 16)

            pipeline(pool, B, (0,), PEEL, step, PERIOD)

        @block.scalar
        def _(act):
            chain = Chain(act, achain)
            act.wait_ge(w_in, 192)
            act.wait_ge(setup, 2)
            act.activation(tg[:, :], gain[:, :], ACT.Tanh).then_inc(vset, 1)
            act.preload_act_table_set("natural_log_exp_and_others")

            def step(p, q, r, z):
                if p:
                    chain.restart()
                    act.wait_ge(stat_done, p.b + 1)
                    chain.done(act.activation(lnv[:, :], mv[:, 1:2], ACT.Ln, bias=eps[:, 0:1]))
                    act.activation(rstd[:, :], lnv[:, :], ACT.Exp, scale=-0.5).then_inc(rstd_done, 1)
                if q:
                    act.wait_ge(n1_done, q.b + 1)
                    act.activation(p1[:, :], bS1[0:T, 0:M], ACT.Exp, bias=n1[:, 0:1], scale=SCALE1, accum_out=l1[:, 0:1]).then_inc(e1_done, 1)
                    act.wait_ge(n2_done, q.b + 1)
                    free(act, p2_done, q.b)
                    for t in range(KT):
                        e = act.activation(p2[:, t, :], bS2[0:KP, t * T:(t + 1) * T], ACT.Exp, bias=n2[:, t:t + 1], scale=SCALE1,
                                           accum_out=l2[:, t:t + 1])
                    e.then_inc(e2_done, 1)
                if z:
                    act.wait_ge(gt_ps, z.b + 1)
                    act.copy(bT[:, :, :].rearrange("p h t -> p (h t)"), bG[:, 0:2 * DH * T]).then_inc(gt_done, 1)
                if p:
                    s = p.slot(2)
                    act.wait_ge(a_ps, p.b + 1)
                    for n, bias in enumerate((g1b, g2b)):
                        for h in range(DH):
                            col = (n * DH + h) * T
                            e = act.activation(aT[:, s, n, h, :], bA[:, col:col + T], ACT.Identity, bias=bias[:, h:h + 1])
                    e.then_inc(a_done, 1)
                if q:
                    act.wait_ge(t1_ps, q.b + 1)
                    act.copy(p1T[:, q.slot(2)].rearrange("p t q -> p (t q)"), bS1[0:KP, 0:KT * T]).then_inc(t1_done, 1)
                if z:
                    act.wait_ge(gl_done, z.b + 1)
                    act.activation(ge[:, :], gl[:, :], ACT.Exp, scale=-1.0).then_inc(ge_done, 1)

            pipeline(act, B, (0, 1, 2, 3), PEEL, step, PERIOD)

        @block.vector
        def _(v):
            chain = Chain(v, vchain)
            v.wait_ge(wset_ps, 1)
            for n, g in enumerate((g1, g2)):
                for h in range(DH):
                    chain.done(v.tensor_copy(g[:, h, :], bank[n][:, h * D:(h + 1) * D]))
            for n, g in enumerate((g1b, g2b, w2)):
                chain.done(v.tensor_copy(g[:, :], bank[2][:, n * DH:(n + 1) * DH]))
            chain.done(v.tensor_copy(bb[:, :], bank[2][0:1, 16:17]))
            v.wait_ge(vset, 1)
            v.sem_inc(vset, 1)

            def step(p, q, r, z):
                if p:
                    b, s = p.b, p.slot(2)
                    chain.restart()
                    v.wait_ge(meta_in[s], 32 * (p.round(2) + 1))
                    chain.done(v.tensor_scalar(wt[:, :], gt[:, s, :], tg[:, 2:3], None, ALU.mult))
                    v.wait_ge(x1_in[s], 16 * (p.round(2) + 1))
                    v.wait_ge(er_in[s], 32 * (p.round(2) + 1))
                    x2b = x2[:, p.slot(4), :]
                    chain.done(v.scalar_tensor_tensor(x2b, er[:, s, 0, :], wt[:, 0:1], x1[:, s, :], ALU.mult, ALU.add))
                    v.scalar_tensor_tensor(x2b, er[:, s, 1, :], wt[:, 1:2], x2b, ALU.mult, ALU.add).then_inc(x2_done, 1)
                    v.wait_ge(x2_done, b + 1)
                    chain.done(v.bn_stats(st[:, :], x2b))
                    v.bn_aggr(mv[:, :], st[:, :]).then_inc(stat_done, 1)
                if q:
                    chain.restart()
                    v.wait_ge(s1_ps, q.b + 1)
                    chain.done(v.reduce_max(m1[:, :], bS1[0:T, 0:M], axis=X_AXIS))
                    v.tensor_scalar(n1[:, :], m1[:, :], -SCALE1, None, ALU.mult).then_inc(n1_done, 1)
                    v.wait_ge(s2_ps, q.b + 1)
                    chain.done(v.reduce_max(m2[:, :], bS2[0:KP, 0:KT * T].rearrange("p (t q) -> p t q", t=KT), axis=X_AXIS))
                    v.tensor_scalar(n2[:, :], m2[:, :], -SCALE1, None, ALU.mult).then_inc(n2_done, 1)
                if p:
                    v.wait_ge(rstd_done, p.b + 1)
                    v.tensor_scalar(xn[:, :], x2[:, p.slot(4), :], mv[:, 0:1], rstd[:, :], ALU.subtract, ALU.mult).then_inc(xn_done, 1)
                if r:
                    chain.restart()
                    v.wait_ge(c_ps, r.b + 1)
                    chain.done(v.tensor_copy(c1T[:, :, :].rearrange("p h t -> p (h t)"), bR[:, 0:DH * T]))
                    v.tensor_copy(p2iT[:, :], bR[0:T, DH * T:(DH + 1) * T]).then_inc(c_done, 1)
                if p:
                    v.wait_ge(xt_ps, p.b + 1)
                    v.tensor_copy(xnT[:, :, :].rearrange("p h t -> p (h t)"), bX[:, 0:DH * T]).then_inc(xnT_done, 1)
                    chain.restart()
                    v.wait_ge(v_ps, p.b + 1)
                    chain.done(v.tensor_scalar(dr[:, p.slot(2), :], bV[0:1, D:D + T], bb[:, :], None, ALU.add))
                    v.tensor_tensor(vc[:, p.slot(4), :], bV[0:T, 0:D], br[:, 1, :], ALU.add).then_inc(v_done, 1)
                if q:
                    s = q.slot(2)
                    chain.restart()
                    v.wait_ge(e1_done, q.b + 1)
                    v.wait_ge(e2_done, q.b + 1)
                    chain.done(v.reciprocal(r1[:, s:s + 1], l1[:, :]))
                    chain.done(v.reciprocal(r2[:, :], l2[:, :]))
                    v.tensor_tensor(p2n[:, s], p2[:, :, :], r2[:, :].unsqueeze(2).broadcast_to((KP, KT, T)), ALU.mult).then_inc(p2_done, 1)
                if r:
                    s = r.slot(2)
                    chain.restart()
                    v.wait_ge(y_ps, r.b + 1)
                    chain.done(v.scalar_tensor_tensor(both[:, s, 0, :], bC[0:T, 0:D], r1[:, s:s + 1], br[:, 0, :], ALU.mult, ALU.add))
                    v.tensor_copy(both[:, s, 1, :], bC[0:T, D:2 * D]).then_inc(y_done, 1)
                if z:
                    s = z.slot(2)
                    c2s, s2c = both[:, s, 0, :], both[:, s, 1, :]
                    chain.restart()
                    v.wait_ge(g_ps, z.b + 1)
                    v.tensor_tensor(gl[:, :], bG[0:T, 0:D], br[:, 2, :], ALU.add).then_inc(gl_done, 1)
                    free(v, x3_done, z.b)
                    chain.done(v.tensor_tensor(df[:, :], c2s, s2c, ALU.subtract))
                    v.wait_ge(ge_done, z.b + 1)
                    chain.done(v.tensor_scalar(gr[:, :], ge[:, :], 1.0, None, ALU.add))
                    chain.done(v.reciprocal(gr[:, :], gr[:, :]))
                    chain.done(v.tensor_tensor(df[:, :], df[:, :], gr[:, :], ALU.mult))
                    chain.done(v.tensor_tensor(df[:, :], df[:, :], s2c, ALU.add))
                    free(v, x3_out[s], 16 * z.round(2))
                    v.scalar_tensor_tensor(x3[:, s, :], df[:, :], tg[:, 1:2], x2[:, z.slot(4), :], ALU.mult, ALU.add).then_inc(x3_done, 1)

            pipeline(v, B, (0, 1, 2, 3), PEEL, step, PERIOD)

        @block.tensor
        def _(pe):
            pe.wait_ge(w_in, 192)
            for n, (left, right) in enumerate(((0, 1), (2, 3))):
                for h in range(DH):
                    for k in range(DH):
                        pe.matmul(bank[n][:, h * D:(h + 1) * D], wraw[:, left, k, h * 128:(h + 1) * 128], wraw[:, right, k, :],
                                  start=k == 0, stop=k == DH - 1)
            for n, (w, c) in enumerate(((1, 0), (3, 2), (2, 3))):
                for h in range(DH):
                    for k in range(DH):
                        pe.matmul(bank[2][:, n * DH + h:n * DH + h + 1], wraw[:, w, k, h * 128:(h + 1) * 128], bc[:, k, c:c + 1],
                                  start=k == 0, stop=k == DH - 1)
            for k in range(DH):
                mm = pe.matmul(bank[2][0:1, 16:17], bc[:, k, 3:4], bc[:, k, 2:3], start=k == 0, stop=k == DH - 1)
            mm.then_inc(wset_ps, 1)
            pe.wait_ge(vset, 2)

            def step(p, q, r, z):
                if q:
                    s = q.slot(2)
                    pe.wait_ge(ct_in[s], 16 * (q.round(2) + 1))
                    pe.wait_ge(a_done, q.b + 1)
                    free(pe, t1_done, q.b)
                    for h in range(DH):
                        mm = pe.matmul(bS1[0:T, 0:M], aT[:, s, 0, h, :], ct[:, s, h, :], start=h == 0, stop=h == DH - 1)
                    mm.then_inc(s1_ps, 1)
                    pe.wait_ge(v_done, q.b + 1)
                    free(pe, e2_done, q.b)
                    for t in range(KT):
                        out = bS2[0:KP, t * T:(t + 1) * T]
                        for h in range(DH):
                            pe.matmul(out, ct[:, s, h, t * KP:(t + 1) * KP], aT[:, s, 1, h, :], start=h == 0, stop=False)
                        mm = pe.matmul(out, onerow[0:1, 0:KP], dr[:, s, :], start=False, stop=True)
                    mm.then_inc(s2_ps, 1)
                if r:
                    s = r.slot(2)
                    pe.wait_ge(t1_done, r.b + 1)
                    pe.wait_ge(p2_done, r.b + 1)
                    pe.wait_ge(cn_in[r.slot(4)], 16 * (r.round(4) + 1))
                    free(pe, c_done, r.b)
                    for h in range(DH):
                        for t in range(KT):
                            pe.matmul(bR[:, h * T:(h + 1) * T], cn[:, r.slot(4), t, h * 128:(h + 1) * 128], p1T[:, s, t, :],
                                      start=t == 0, stop=t == KT - 1)
                    for t in range(KT):
                        mm = pe.matmul(bR[0:T, DH * T:(DH + 1) * T], p2n[:, s, t, :], win[:, t, :], start=t == 0, stop=t == KT - 1)
                    mm.then_inc(c_ps, 1)
                if p:
                    pe.wait_ge(xn_done, p.b + 1)
                    free(pe, xnT_done, p.b)
                    for h in range(DH):
                        mm = pe.transpose(bX[:, h * T:(h + 1) * T], xn[:, h * 128:(h + 1) * 128], ident[0:T, 0:T])
                    mm.then_inc(xt_ps, 1)
                if z:
                    s = z.slot(2)
                    pe.wait_ge(y_done, z.b + 1)
                    free(pe, gl_done, z.b)
                    for n in range(2):
                        for h in range(DH):
                            col = (n * DH + h) * T
                            mm = pe.transpose(bG[:, col:col + T], both[:, s, n, h * 128:(h + 1) * 128], ident[0:T, 0:T])
                    mm.then_inc(gt_ps, 1)
                if p:
                    pe.wait_ge(xnT_done, p.b + 1)
                    free(pe, a_done, p.b)
                    for n, g in enumerate((g1, g2)):
                        for h in range(DH):
                            for k in range(DH):
                                mm = pe.matmul(bA[:, (n * DH + h) * T:(n * DH + h + 1) * T], g[:, k, h * 128:(h + 1) * 128], xnT[:, k, :],
                                               start=k == 0, stop=k == DH - 1)
                    mm.then_inc(a_ps, 1)
                    free(pe, v_done, p.b)
                    for k in range(DH):
                        pe.matmul(bV[0:T, 0:D], xnT[:, k, :], wvc[:, k, :], start=k == 0, stop=k == DH - 1)
                    for k in range(DH):
                        mm = pe.matmul(bV[0:1, D:D + T], w2[:, k:k + 1], xnT[:, k, :], start=k == 0, stop=k == DH - 1)
                    mm.then_inc(v_ps, 1)
                if r:
                    pe.wait_ge(c_done, r.b + 1)
                    free(pe, y_done, r.b)
                    for h in range(DH):
                        pe.matmul(bC[0:T, 0:D], c1T[:, h, :], wvs[:, h, :], start=h == 0, stop=h == DH - 1)
                    pe.matmul(bC[0:T, D:2 * D], p2iT[:, :], vc[:, r.slot(4), :], start=True, stop=True).then_inc(y_ps, 1)
                if q:
                    pe.wait_ge(e1_done, q.b + 1)
                    for t in range(KT):
                        mm = pe.transpose(bS1[0:KP, t * T:(t + 1) * T], p1[:, t * KP:(t + 1) * KP], ident[0:T, 0:T])
                    mm.then_inc(t1_ps, 1)
                if z:
                    pe.wait_ge(gt_done, z.b + 1)
                    for k in range(2 * DH):
                        mm = pe.matmul(bG[0:T, 0:D], bT[:, k, :], wg[:, k, :], start=k == 0, stop=k == 2 * DH - 1)
                    mm.then_inc(g_ps, 1)

            pipeline(pe, B, (0, 1, 2, 3), PEEL, step, PERIOD)

        work.close()
        at_rest(nc, signals)




PH, PK, KEYS, DK = 8, 8, 64, 128
PAIR = B // 2
SETS = PH * 2
NC = KEYS * KEYS // 128
GO = 8
TG, CG = T // GO, NC // GO
RMS_EPS = 1e-6


def retrieve(nc, x3_d, wq, keysT, downT, up, norm, gates, consts, out_d):
    ctx, work = ExitStack(), ExitStack()
    with ctx:
        def sb(name, shape, dt=F32):
            return ctx.enter_context(nc.sbuf_tensor(name, shape, dt))

        def sem(name):
            signals.append(ctx.enter_context(nc.semaphore(name)))
            return signals[-1]

        signals = []

        cst = sb("cst_d", [128, 512])
        ident, iota = cst[:, 0:128], cst[:, 352:480]
        gain, tg, eps = sb("gain_d", [T, 4]), sb("tg_d", [T, 4]), sb("eps_d", [T, 2])
        nw = sb("nw", [T, D])
        dT = sb("dT", [128, DH, NC, 128])
        u_s = sb("u_s", [128, NC, D])
        cw = sb("cw", [128, DH, SETS * KEYS])
        g = sb("g", [128, 2, NC, 2 * T])
        wq_s = g[:, 0, :, :].rearrange("p c t -> p (c t)")[:, 0:SETS * D].rearrange("p (s d) -> p s d", s=SETS)
        ks = g[:, 1, :, :].rearrange("p c t -> p (c t)")[:, 0:SETS * KEYS].rearrange("p (s k) -> p s k", s=SETS)
        xs, xl = sb("xs", [T, 2, 2, D]), sb("xl", [T, 2, D])
        st, mv, lnv, rstd = sb("st_d", [T, 2, 6]), sb("mv_d", [T, 2, 2]), sb("lnv_d", [T, 2]), sb("rstd_d_s", [T, 2])
        sq, ms, inv = sb("sq", [T, D]), sb("ms", [T, 2]), sb("inv", [T, 2])
        xnT = sb("xnT_d", [128, 2, DH, 2 * T])
        sim = sb("sim", [T, 2, 2, SETS * KEYS])
        val = sb("val", [T, 2 * SETS, 8])
        idx = sb("idx", [T, 2 * SETS, 8], U32)
        idxf = sb("idxf", [T, 2 * SETS, 8])
        cand = sb("cand", [T, 2 * PH, PK * PK])
        best = sb("best", [T, 2 * PH, PK])
        ci = sb("ci", [T, 2 * PH, PK], U32)
        cab = sb("cab", [T, 2, 2 * PH, PK], U32)
        cabf = sb("cabf", [T, 2, 2 * PH, PK])
        eq = sb("eq", [T, 2, 2 * PH, PK, 8])
        ij = sb("ij", [T, 2, 2 * PH * PK])
        kin = sb("kin", [T, 3, 2 * PH * PK])
        ef, ei = sb("ef", [T, 2 * PH * PK]), sb("ei", [T, 2, 2 * PH * PK], I32)
        pc = sb("pc", [128, 2, T])
        rp = sb("rp", [128, T, 3], BF16)
        rrest = sb("rrest", [128, T])
        hotp = sb("hotp", [128, 2, TG, 128], BF16)
        hotc = sb("hotc", [128, 2, TG, NC], BF16)
        hotw = sb("hotw", [128, 2, TG, 3, NC], BF16)
        xr = sb("xr_d", [T, 2, 2, D])
        y = sb("y_d", [T, 2, 2, D])

        bank = [ctx.enter_context(nc.psum_tensor(f"dbank{i}", [128, 512], F32)) for i in range(4)]
        wbank = [ctx.enter_context(nc.psum_tensor(f"wbank{i}", [128, 2, 512], F32)) for i in range(2)]
        bM, bD, bU = bank[0], bank[1], bank[2:4]

        w_in, setup, vset, cset_ps, cset_done, spass, gpass, vpass = (
            sem(n + "_d") for n in "w_in setup vset cset_ps cset_done spass gpass vpass".split())
        x_in = [sem(f"x_in_d{s}") for s in range(2)]
        xr_in = [sem(f"xr_in_d{s}") for s in range(2)]
        y_out = [sem(f"y_out_d{s}") for s in range(2)]
        (stat_done, rstd_done, xl_done, inv_done, xn_done, xt_ps, xnT_done, sim_ps, sim_done, val_done, best_done, kin_done,
         kt_ps, kt_done, hp_done, hc_done, w_ps, w_done, d_ps, g_done, u_ps, y_done, up_go, oc_done, ij_done) = (sem(n + "_p") for n in (
             "stat_done rstd_done xl_done inv_done xn_done xt_ps xnT_done sim_ps sim_done val_done best_done kin_done "
             "kt_ps kt_done hp_done hc_done w_ps w_done d_ps g_done u_ps y_done up_go oc_done ij_done").split())
        vchain, achain, gchain = sem("vchain_d"), sem("achain_d"), sem("gchain_d")
        block = work.enter_context(nc.Block())
        PEEL = 6
        x3_v = x3_d.rearrange("(u t) p d -> u p t d", t=2)
        out_v = out_d.rearrange("(u t) p d -> u p t d", t=2)

        def pair(ap, b):
            return ap[bass.ds(b, 1)].rearrange("a p t d -> p (a t) d")

        def upto(value, most):
            return min(value, most) if isinstance(value, int) else value

        @block.sync
        def _(sp):
            def need(signal, value):
                if not (isinstance(value, int) and value <= 0):
                    hold(sp, signal, value, spass)

            sp.dma_start(cst[:, :], consts).then_inc(w_in, 16)
            sp.dma_start(gain[:, :], gates).then_inc(w_in, 16)
            sp.dma_start(nw[:, :], norm).then_inc(w_in, 16)
            sp.dma_start(wq_s, wq.rearrange("(s p) d -> p s d", p=DK)).then_inc(w_in, 16)
            sp.dma_start(ks, keysT).then_inc(w_in, 16)
            sp.dma_start(dT[:, :, :, :], downT.rearrange("(h p) c e -> p h c e", p=128)).then_inc(w_in, 16)
            sp.dma_start(u_s[:, :, :], up.rearrange("(p c) d -> p c d", p=128)).then_inc(w_in, 16)

            def step(load, out):
                if load:
                    b, s = load.b, load.slot(2)
                    need(xl_done, b - 1)
                    sp.dma_start(xs[:, s], pair(x3_v, b)).then_inc(x_in[s], 16)
                if out:
                    b, s = out.b, out.slot(2)
                    need(y_done, b - 1)
                    sp.dma_start(xr[:, s], pair(x3_v, b)).then_inc(xr_in[s], 16)
                    need(y_done, b + 1)
                    sp.dma_start(pair(out_v, b), y[:, s]).then_inc(y_out[s], 16)

            pipeline(sp, PAIR, (0, 4), PEEL, step)
            for s in range(2):
                sp.wait_ge(y_out[s], 16 * (PAIR // 2))

        @block.gpsimd
        def _(pool):
            chain = Chain(pool, gchain)
            chain.done(pool.memset(eps[:, 0:1], LN_EPS))
            chain.done(pool.memset(eps[:, 1:2], RMS_EPS))
            pool.sem_inc(setup, 1)
            pool.wait_ge(w_in, 112)

            def step(k, w):
                if w:
                    for n in range(GO):
                        at_n = w.b * GO + n
                        toks = slice(n * TG, (n + 1) * TG)
                        hold(pool, oc_done, at_n + 1, gpass)
                        if not (isinstance(at_n, int) and at_n < 2):
                            hold(pool, w_ps, at_n - 1, gpass)
                        pool.tensor_tensor(hotw[:, n % 2], hotc[:, n % 2].unsqueeze(2).broadcast_to((128, TG, 3, NC)),
                                           rp[:, toks, :].unsqueeze(3).broadcast_to((128, TG, 3, NC)), ALU.mult).then_inc(hc_done, 1)
                        pool.wait_ge(hc_done, at_n + 1)
                if k:
                    hold(pool, best_done, k.b + 1, gpass)
                    chain.restart()
                    for half in range(2):
                        found = idxf[:, :, :].rearrange("p (s a) k -> p s a k", a=2)[:, :, half, :].unsqueeze(2).broadcast_to((T, 2 * PH, PK, 8))
                        ins = pool.tensor_tensor(eq[:, half], eq[:, half], found, ALU.mult)
                        if half == 0:
                            chain.done(ins)
                    ins.then_inc(ij_done, 1)
                    pool.wait_ge(ij_done, k.b + 1)

            pipeline(pool, PAIR, (1, 2), PEEL, step)

        @block.scalar
        def _(act):
            chain = Chain(act, achain)
            act.wait_ge(w_in, 112)
            act.wait_ge(setup, 1)
            act.activation(tg[:, :], gain[:, :], ACT.Tanh).then_inc(vset, 1)

            def step(p, d):
                if p:
                    act.preload_act_table_set("natural_log_exp_and_others")
                    chain.restart()
                    act.wait_ge(stat_done, p.b + 1)
                    chain.done(act.activation(lnv[:, :], mv[:, :, 1], ACT.Ln, bias=eps[:, 0:1]))
                    act.activation(rstd[:, :], lnv[:, :], ACT.Exp, scale=-0.5).then_inc(rstd_done, 1)
                    act.wait_ge(xl_done, p.b + 1)
                    for t in range(2):
                        chain.done(act.activation(sq[:, :], xl[:, t, :], ACT.Square, accum_out=ms[:, t:t + 1]))
                    chain.done(act.activation(ms[:, :], ms[:, :], ACT.Ln, bias=eps[:, 1:2], scale=1.0 / D))
                    act.activation(inv[:, :], ms[:, :], ACT.Exp, scale=-0.5).then_inc(inv_done, 1)
                    act.preload_act_table(ACT.Gelu)
                for n in range(GO):
                    if d:
                        for u in range(2):
                            at_u = (d.b * GO + n) * 2 + u
                            c = n * CG + 2 * u
                            act.wait_ge(d_ps, at_u + 1)
                            act.activation(g[:, d.slot(2), c:c + 2, :].rearrange("p c t -> p (c t)"), bD[:, 0:4 * T], ACT.Gelu).then_inc(g_done, 1)
                    if p and n == 2:
                        act.wait_ge(xt_ps, p.b + 1)
                        act.copy(xnT[:, p.slot(2)].rearrange("p h t -> p (h t)"), bM[:, 0:4 * T]).then_inc(xnT_done, 1)
                    if p and 3 <= n < 7:
                        q = n - 3
                        act.wait_ge(sim_ps, p.b * 4 + q + 1)
                        free(act, val_done, p.b - 1)
                        act.copy(sim[:, p.slot(2), q // 2, (q % 2) * 512:(q % 2 + 1) * 512], bM[0:T, 0:512]).then_inc(sim_done, 1)

            pipeline(act, PAIR, (0, 1), PEEL, step)

        @block.vector
        def _(v):
            chain = Chain(v, vchain)
            v.wait_ge(cset_ps, 1)
            for n, src in enumerate((wbank[0][:, 0, :], wbank[0][:, 1, :], wbank[1][:, 0, :], wbank[1][:, 1, :])):
                chain.done(v.tensor_copy(cw[:, n // 2, (n % 2) * 512:(n % 2 + 1) * 512], src))
            v.wait_ge(vset, 1)
            v.sem_inc(cset_done, 1)
            FIRST = [(0, 7), (7, 14), (14, 20), (20, 26), (26, 32)]

            def step(p, k, w, up):
                if p:
                    b, s = p.b, p.slot(2)
                    chain.restart()
                    v.wait_ge(x_in[s], 16 * (p.round(2) + 1))
                    for t in range(2):
                        chain.done(v.bn_stats(st[:, t], xs[:, s, t, :]))
                    chain.done(v.bn_aggr(mv[:, 0], st[:, 0]))
                    v.bn_aggr(mv[:, 1], st[:, 1]).then_inc(stat_done, 1)
                if w:
                    chain.restart()
                    v.wait_ge(ij_done, w.b + 1)
                    chain.done(v.reduce_sum(ij[:, :, :].rearrange("p a s -> p (a s)"), eq[:, :, :, :, :].rearrange("p a s k n -> p (a s k) n"), axis=X_AXIS))
                    chain.done(v.scalar_tensor_tensor(ef[:, :], ij[:, 0, :], float(KEYS), ij[:, 1, :], ALU.mult, ALU.add))
                    chain.done(v.tensor_copy(ei[:, 0, :], ef[:, :]))
                    chain.done(v.tensor_scalar(ei[:, 1, :], ei[:, 0, :], NC - 1, None, ALU.bitwise_and))
                    chain.done(v.tensor_scalar(ei[:, 0, :], ei[:, 0, :], NC.bit_length() - 1, None, ALU.logical_shift_right))
                    chain.done(v.tensor_scalar(kin[:, 2, :], best[:, :, :].rearrange("p s k -> p (s k)"), 0.0, None, ALU.max))
                    v.tensor_copy(kin[:, 0:2, :], ei[:, :, :]).then_inc(kin_done, 1)
                    v.wait_ge(kt_ps, w.b + 1)
                    chain.done(v.tensor_copy(pc[:, :, :].rearrange("p n t -> p (n t)"), bM[:, 0:2 * T]))
                    chain.done(v.tensor_copy(rp[:, :, 0], bM[:, 2 * T:3 * T]))
                    chain.done(v.tensor_tensor(rrest[:, :], bM[:, 2 * T:3 * T], rp[:, :, 0], ALU.subtract))
                    chain.done(v.tensor_copy(rp[:, :, 1], rrest[:, :]))
                    v.tensor_tensor(rp[:, :, 2], rrest[:, :], rp[:, :, 1], ALU.subtract).then_inc(kt_done, 1)
                for n in range(GO):
                    if w:
                        at_n = w.b * GO + n
                        v.wait_ge(kt_done, w.b + 1)
                        free(v, hc_done, at_n - 1)
                        v.tensor_tensor(hotc[:, n % 2], iota[:, 0:NC].unsqueeze(1).broadcast_to((128, TG, NC)),
                                        pc[:, 1, n * TG:(n + 1) * TG].unsqueeze(2).broadcast_to((128, TG, NC)), ALU.is_equal).then_inc(oc_done, 1)
                        free(v, w_ps, at_n - 1)
                        v.tensor_tensor(hotp[:, n % 2], iota.unsqueeze(1).broadcast_to((128, TG, 128)),
                                        pc[:, 0, n * TG:(n + 1) * TG].unsqueeze(2).broadcast_to((128, TG, 128)), ALU.is_equal).then_inc(hp_done, 1)
                    if p and n == 0:
                        s = p.slot(2)
                        chain.restart()
                        v.wait_ge(rstd_done, p.b + 1)
                        chain.done(v.tensor_scalar(xl[:, 0, :], xs[:, s, 0, :], mv[:, 0, 0:1], rstd[:, 0:1], ALU.subtract, ALU.mult))
                        v.tensor_scalar(xl[:, 1, :], xs[:, s, 1, :], mv[:, 1, 0:1], rstd[:, 1:2], ALU.subtract, ALU.mult).then_inc(xl_done, 1)
                    if p and n == 1:
                        chain.restart()
                        v.wait_ge(inv_done, p.b + 1)
                        chain.done(v.scalar_tensor_tensor(xl[:, 0, :], xl[:, 0, :], inv[:, 0:1], nw[:, :], ALU.mult, ALU.mult))
                        v.scalar_tensor_tensor(xl[:, 1, :], xl[:, 1, :], inv[:, 1:2], nw[:, :], ALU.mult, ALU.mult).then_inc(xn_done, 1)
                    if k:
                        s = k.slot(2)
                        chain.restart()
                        if n == 0:
                            hold(v, sim_done, (k.b + 1) * 4, vpass)
                        if n < len(FIRST):
                            for q in range(*FIRST[n]):
                                row = sim[:, s, q // SETS, (q % SETS) * KEYS:(q % SETS + 1) * KEYS]
                                chain.done(v.max(val[:, q, :], row))
                                chain.done(v.max_index(idx[:, q, :], val[:, q, :], row))
                        if n == 5:
                            v.sem_inc(val_done, 1)
                            chain.done(v.tensor_copy(idxf[:, :, :], idx[:, :, :]))
                            both = val[:, :, :].rearrange("p (s a) k -> p s a k", a=2)
                            chain.done(v.tensor_tensor(cand[:, :, :].rearrange("p s (a b) -> p s a b", a=PK),
                                                       both[:, :, 0, :].unsqueeze(3).broadcast_to((T, 2 * PH, PK, PK)),
                                                       both[:, :, 1, :].unsqueeze(2).broadcast_to((T, 2 * PH, PK, PK)), ALU.add))
                        if n in (5, 6):
                            for q in range((n - 5) * PH, (n - 4) * PH):
                                chain.done(v.max(best[:, q, :], cand[:, q, :]))
                                chain.done(v.max_index(ci[:, q, :], best[:, q, :], cand[:, q, :]))
                        if n == 6:
                            chain.done(v.tensor_scalar(cab[:, 0], ci[:, :, :], 3, None, ALU.logical_shift_right))
                            chain.done(v.tensor_scalar(cab[:, 1], ci[:, :, :], 7, None, ALU.bitwise_and))
                            chain.done(v.tensor_copy(cabf[:, :, :, :], cab[:, :, :, :]))
                            for half in range(2):
                                ins = v.tensor_tensor(eq[:, half], iota[0:T, 0:8].unsqueeze(1).unsqueeze(1).broadcast_to((T, 2 * PH, PK, 8)),
                                                      cabf[:, half].unsqueeze(3).broadcast_to((T, 2 * PH, PK, 8)), ALU.is_equal)
                            ins.then_inc(best_done, 1)
                    if w:
                        if n == 0:
                            v.wait_ge(g_done, (w.b + 1) * 2 * GO)
                        v.wait_ge(w_ps, at_n + 1)
                        here = g[:, w.slot(2)].rearrange("p c (t n) -> p t c n", t=2)[:, :, :, n * TG:(n + 1) * TG]
                        v.tensor_tensor(here, wbank[n % 2][:, :, 0:TG * NC].rearrange("p t (n c) -> p t c n", n=TG), here, ALU.mult).then_inc(w_done, 1)
                if up:
                    s = up.slot(2)
                    chain.restart()
                    v.wait_ge(u_ps, up.b + 1)
                    v.wait_ge(xr_in[s], 16 * (up.round(2) + 1))
                    free(v, y_out[s], 16 * up.round(2))
                    chain.done(v.scalar_tensor_tensor(y[:, s, 0, :], bU[0][0:T, 0:D], tg[:, 3:4], xr[:, s, 0, :], ALU.mult, ALU.add))
                    v.scalar_tensor_tensor(y[:, s, 1, :], bU[1][0:T, 0:D], tg[:, 3:4], xr[:, s, 1, :], ALU.mult, ALU.add).then_inc(y_done, 1)

            pipeline(v, PAIR, (0, 1, 2, 3), PEEL, step)

        @block.tensor
        def _(pe):
            pe.wait_ge(w_in, 112)
            for h in range(DH):
                for q in range(SETS):
                    mm = pe.matmul(wbank[h][:, q // 8, (q % 8) * KEYS:(q % 8 + 1) * KEYS], wq_s[:, q, h * 128:(h + 1) * 128], ks[:, q, :],
                                   start=True, stop=True)
            mm.then_inc(cset_ps, 1)
            pe.wait_ge(cset_done, 1)

            def step(p, d, w, up):
                if w:
                    pe.wait_ge(kin_done, w.b + 1)
                    pe.wait_ge(sim_done, upto((w.b + 2) * 4, PAIR * 4))
                    for n in range(3):
                        mm = pe.transpose(bM[:, n * T:(n + 1) * T], kin[:, n, :], ident[0:T, 0:T])
                    mm.then_inc(kt_ps, 1)
                for n in range(GO):
                    if up:
                        s = up.slot(2)
                        if n == 0:
                            pe.wait_ge(w_done, (up.b + 1) * GO)
                            free(pe, y_done, up.b)
                        for c in range(n * CG, (n + 1) * CG):
                            for t in range(2):
                                mm = pe.matmul(bU[t][0:T, 0:D], g[:, s, c, t * T:(t + 1) * T], u_s[:, c, :], start=c == 0, stop=c == NC - 1)
                        if n == GO - 1:
                            mm.then_inc(u_ps, 1)
                        else:
                            mm.then_inc(up_go, 1)
                    for u in range(2):
                        if d:
                            s = d.slot(2)
                            at_u = (d.b * GO + n) * 2 + u
                            if n == 0 and u == 0:
                                pe.wait_ge(xnT_done, d.b + 1)
                            free(pe, g_done, at_u)
                            for cc in range(2):
                                c = n * CG + 2 * u + cc
                                for h in range(DH):
                                    mm = pe.matmul(bD[:, cc * 2 * T:(cc + 1) * 2 * T], dT[:, h, c, :], xnT[:, s, h, :], start=h == 0, stop=h == DH - 1)
                            mm.then_inc(d_ps, 1)
                        if w:
                            at_n = w.b * GO + n
                            if u == 0:
                                pe.wait_ge(hp_done, at_n + 1)
                                pe.wait_ge(hc_done, at_n + 1)
                                free(pe, w_done, at_n - 1)
                            rows = slice(u * 64, u * 64 + 64)
                            for tok in range(TG):
                                for part in range(3):
                                    mm = pe.matmul(wbank[n % 2][:, u, tok * NC:(tok + 1) * NC], hotp[rows, n % 2, tok, :], hotw[rows, n % 2, tok, part, :],
                                                   start=part == 0, stop=part == 2)
                            if u == 1:
                                mm.then_inc(w_ps, 1)
                    if p and n == 2:
                        pe.wait_ge(xn_done, p.b + 1)
                        free(pe, kt_done, p.b - 1)
                        free(pe, sim_done, p.b * 4)
                        for h in range(DH):
                            for t in range(2):
                                mm = pe.transpose(bM[:, (h * 2 + t) * T:(h * 2 + t + 1) * T], xl[:, t, h * 128:(h + 1) * 128], ident[0:T, 0:T])
                        mm.then_inc(xt_ps, 1)
                    if p and 3 <= n < 7:
                        q = n - 3
                        if q == 0:
                            pe.wait_ge(xnT_done, p.b + 1)
                        free(pe, sim_done, p.b * 4 + q)
                        for h in range(DH):
                            mm = pe.matmul(bM[0:T, 0:512], xnT[:, p.slot(2), h, (q // 2) * T:(q // 2 + 1) * T],
                                           cw[:, h, (q % 2) * 512:(q % 2 + 1) * 512], start=h == 0, stop=h == DH - 1)
                        mm.then_inc(sim_ps, 1)

            pipeline(pe, PAIR, (0, 1, 2, 3), PEEL, step)

        work.close()
        at_rest(nc, signals)




DEBUG = False
_OUTS = [((B, T, D), "float32")]


def kernel(**inputs):
    import numpy as np
    import concourse.bacc as _bacc
    from concourse import mybir as _mybir
    from concourse.bass_utils import run_bass_kernel_spmd as _run

    I = inputs
    rows = lambda a: np.ascontiguousarray(np.broadcast_to(a, (T, a.shape[-1])))
    lay = {
        "x": I["x"], "ctxT": I["ctx_1024"].transpose(0, 2, 1),
        "wq": I["L0_xattn_Wq"], "wk": I["L0_xattn_Wk"], "wv": I["L0_xattn_Wv"], "wp": I["L0_xattn_Wp"],
        "bp": rows(I["L0_xattn_bp"]), "wg": I["L0_ffn_Wg"].T,
        "w1": I["L0_ffn_W1"], "w2": I["L0_ffn_W2"],
        "ctx": I["ctx_1024"], "wqc": I["L1_xattn_Wq_c"], "wks": I["L1_xattn_Wk_s"], "wkc": I["L1_xattn_Wk_c"], "wqs": I["L1_xattn_Wq_s"],
        "wvsT": I["L1_xattn_Wv_s"].T, "wvcT": I["L1_xattn_Wv_c"].T, "wgT": I["L1_xattn_Wg"].T,
        "bcols": np.stack([I["L1_xattn_bq_c"], I["L1_xattn_bk_s"], I["L1_xattn_bk_c"], I["L1_xattn_bq_s"]], axis=1),
        "brows": np.broadcast_to(np.stack([I["L1_xattn_bv_s"], I["L1_xattn_bv_c"], I["L1_xattn_bg"]]), (T, 3, D)),
        "pwq": I["L1_ffn_w_q"], "keysT": I["L1_ffn_keys"].transpose(3, 0, 2, 1).reshape(DK, SETS, KEYS),
        "downT": I["L1_ffn_expert_down"].reshape(128, NC, D).transpose(2, 1, 0), "up": I["L1_ffn_expert_up"],
        "norm": rows(I["L1_ffn_norm_w"]),
        "gates": rows(np.concatenate([I["g_xattn"], I["g_ffn"]])),
    }
    consts = np.zeros((128, 512), np.float32)
    consts[:, 0:128] = np.eye(128)
    consts[0:T, 128:128 + T] = np.triu(np.ones((T, T)), 1)
    consts[:, 240:240 + T] = 1.0
    consts[:, 352:480] = np.arange(128)
    where = np.clip((np.arange(T, dtype=np.float32) + np.float32(0.5)) * np.float32(M / T) - np.float32(0.5), 0, M - 1).astype(np.float32)
    low = np.floor(where).astype(np.int64)
    share = where - low.astype(np.float32)
    weight = np.zeros((M, T), np.float32)
    weight[low, np.arange(T)] += 1 - share
    weight[np.minimum(low + 1, M - 1), np.arange(T)] += share
    lay["interp"] = weight.reshape(KT, KP, T).transpose(1, 0, 2)
    lay["consts"] = consts
    nc = _bacc.Bacc("TRN2", target_bir_lowering=False, num_devices=1)
    arrays, aps = {}, {}
    for name, a in lay.items():
        a = np.ascontiguousarray(a)
        arrays[f"in_{name}"] = a
        aps[name] = nc.dram_tensor(f"in_{name}", a.shape, _mybir.dt.from_np(a.dtype), kind="ExternalInput").ap()
    K = "ExternalOutput"
    def scratch(name, shape, dt=F32, debug=False):
        return nc.dram_tensor(name, shape, dt, kind="ExternalOutput" if debug else "Internal").ap()
    x1_d = scratch("x1_d", (B, T, D), debug=DEBUG)
    disp_d = scratch("disp_d", (E * CAP, D), debug=DEBUG)
    slot_d = scratch("slot_d", (B, T, 2), I32, debug=DEBUG)
    gate_d = scratch("gate_d", (B, T, 2), debug=DEBUG)
    kst_d = [scratch(f"kstage{s}", (3 * D, M), BF16) for s in range(2)]
    qst_d = [scratch(f"qstage{s}", (3 * D, T), BF16) for s in range(2)]
    mst_d = [scratch(f"mstage{s}", (H, 3 * T), BF16) for s in range(2)]
    attend(nc, aps["x"], aps["ctxT"], aps["wq"], aps["wk"], aps["wv"], aps["wp"], aps["bp"], aps["wg"], aps["gates"], aps["consts"],
           x1_d, disp_d, slot_d, gate_d, kst_d, qst_d, mst_d)
    eout_d = scratch("eout_d", (E * CAP, D), debug=DEBUG)
    experts(nc, aps["w1"], aps["w2"], aps["consts"], disp_d, eout_d)
    x3_d = scratch("x3_d", (B, T, D), debug=DEBUG)
    cross(nc, x1_d, eout_d, slot_d, gate_d, aps["ctxT"], aps["ctx"], aps["wqc"], aps["wks"], aps["wkc"], aps["wqs"], aps["wvsT"], aps["wvcT"],
          aps["wgT"], aps["bcols"], aps["brows"], aps["gates"], aps["consts"], aps["interp"], None, x3_d)
    out_d = nc.dram_tensor("out_0", (B, T, D), F32, kind="ExternalOutput").ap()
    retrieve(nc, x3_d, aps["pwq"], aps["keysT"], aps["downT"], aps["up"], aps["norm"], aps["gates"], aps["consts"], out_d)
    r = _run(nc, [arrays], core_ids=[0])
    return r.results[0]["out_0"]
```

```python
import concourse.bass as bass
from concourse import mybir
from concourse.alu_op_type import AluOpType as ALU
from contextlib import ExitStack

F32 = mybir.dt.float32
BF16 = mybir.dt.bfloat16
I32 = mybir.dt.int32
U32 = mybir.dt.uint32
ACT = mybir.ActivationFunctionType
X_AXIS = mybir.AxisListType.X

B, T, D, M = 32, 112, 256, 375
DH = D // 128
KT = 3
KP = M // KT
H, HD = 16, 16
SCALE0 = HD ** -0.5
HPT = 128 // HD
E = 8
CAP = int(B * T * 2 * 1.25 / E)
FF = 512
LN_EPS = 1e-5
PAIRS = [(0, 0), (0, 1), (0, 2), (1, 0), (1, 1), (2, 0)]
STACK = len(PAIRS) * HD
NST = STACK + 3


class Chain:

    def __init__(self, eng, sem):
        self.eng, self.sem, self.n = eng, sem, 0

    def restart(self):
        self.eng.sem_clear(self.sem)
        self.n = 0

    def done(self, ins):
        ins.then_inc(self.sem, 1)
        self.n += 1
        self.eng.wait_ge(self.sem, self.n)


def hold(eng, sem, value, passed):
    eng.wait_ge(sem, value)
    eng.sem_inc(passed, 1)


class Tile:

    def __init__(self, rounds, place, period):
        self.rounds, self.place, self.period = rounds, place, period
        self.b = rounds * period + place

    def slot(self, n):
        return self.place % n

    def round(self, n):
        return self.rounds * (self.period // n) + self.place // n


def pipeline(eng, count, lags, peel, step, period=2):
    def tiles(n):
        return [Tile((n - lag) // period, (n - lag) % period, period) if 0 <= n - lag < count else None for lag in lags]
    for n in range(peel):
        step(*tiles(n))
    with eng.Fori(peel // period, count // period) as i:
        for n in range(period):
            step(*[Tile(i + (n - lag) // period, (n - lag) % period, period) for lag in lags])
    for n in range(count, count + max(lags)):
        step(*tiles(n))


def free(eng, sem, value):
    if not (isinstance(value, int) and value <= 0):
        eng.wait_ge(sem, value)


def upto(value, most):
    return min(value, most) if isinstance(value, int) else value


def at(ap, index):
    return ap[bass.ds(index, 1), :, :].rearrange("a p d -> p (a d)")


def at_rest(nc, signals):
    numbers = sorted(s.num for s in signals)
    first = [n for n in numbers if n - 1 not in numbers]
    last = [n for n in numbers if n + 1 not in numbers]
    with nc.Block() as block:
        @block.sync
        def _(sp):
            for lo, hi in zip(first, last):
                sp.sem_clear(range(lo, hi + 1))


def attend(nc, x, ctxT, wq, wk, wv, wp, bp, wg, gates, consts, x1_d, disp_d, slot_d, gate_d, kstage_d, qstage_d, mstage_d):
    ctx, work = ExitStack(), ExitStack()
    with ctx:
        def sb(name, shape, dt=F32):
            return ctx.enter_context(nc.sbuf_tensor(name, shape, dt))

        def sem(name):
            signals.append(ctx.enter_context(nc.semaphore(name)))
            return signals[-1]

        signals = []

        wq_s = sb("wq_s", [128, DH, D])
        wk_s = sb("wk_s", [128, DH, D])
        wv_s = sb("wv_s", [128, DH, D])
        wp_s = sb("wp_s", [128, DH, D])
        wg_s = sb("wg_s", [128, DH, E])
        cst = sb("cst", [128, 512])
        ident, before, ones, iota = cst[:, 0:128], cst[:, 128:128 + T], cst[:, 240:240 + T], cst[:, 352:480]
        gain = sb("gain", [T, 4])
        tg = sb("tg", [T, 4])
        bias = sb("bias", [T, D])
        eps = sb("eps", [T, 1])
        zeros = sb("zeros", [T, 2560])
        ct = sb("ct", [128, 2, DH, M])
        xt = sb("xt", [T, 2, D])
        stats = sb("stats", [T, 6])
        mv = sb("mv", [T, 2, 2])
        lnv = sb("lnv", [T, 2])
        rstd = sb("rstd", [T, 2])
        xn = sb("xn", [T, 2, D])
        xnT = sb("xnT", [128, 2, DH, T])
        kpart = sb("kpart", [128, 2, 3, DH, M], BF16)
        krest = sb("krest", [128, 2, DH, M])
        qpart = sb("qpart", [128, 2, 3, DH, T], BF16)
        qrest = sb("qrest", [128, 2, DH, T])
        vt = sb("vt", [KP, 4, KT, H, HD + 1])
        kst = sb("kst", [NST, 4, H, M], BF16)
        qst = sb("qst", [NST, 4, H, T], BF16)
        mx = sb("mx", [T, 2, H])
        mneg = sb("mneg", [H, T])
        mrest = sb("mrest", [H, T])
        mpart = sb("mpart", [H, 2, 3, T], BF16)
        probs = sb("probs", [KP, 2, KT, H * T])
        den = sb("den", [T, H])
        o = sb("o", [T, H, HD])
        oT = sb("oT", [128, DH, T])
        xr = sb("xr", [T, 2, D])
        x1 = sb("x1", [T, 2, D])
        st2 = sb("st2", [T, 6])
        mv2 = sb("mv2", [T, 2])
        lnv2 = sb("lnv2", [T, 1])
        rstd2 = sb("rstd2", [T, 1])
        xn2 = sb("xn2", [T, 2, D])
        xn2T = sb("xn2T", [128, DH, T])
        lg = sb("lg", [T, E])
        best = sb("best_a", [T, 8])
        topi = sb("topi", [T, 8], U32)
        topf = sb("topf", [T, 8])
        hot = sb("hot", [T, 2, E])
        cnt = sb("cnt", [T, E])
        total = sb("total", [T, E])
        pos = sb("pos", [T, 2, E])
        pos2 = sb("pos2", [T, 2])
        slotf = sb("slotf", [T, 2])
        over = sb("over", [T, 2])
        sent = sb("sent", [T, 2, 2], I32)
        fetch = sb("fetch", [T, 2, 2], I32)
        gx = sb("gx", [T, 2])
        gt = sb("gt", [T, 2, 2])

        bank = [ctx.enter_context(nc.psum_tensor(f"bank{i}", [128, 512], F32)) for i in range(8)]
        pT, pQ = bank[0][:, 0:DH * T], bank[0][:, DH * T:2 * DH * T]
        pR = bank[0][0:T, 2 * DH * T:2 * DH * T + E]
        pKV, pS, pE, pO = bank[1:3], bank[3:5], bank[5:7], bank[7]

        weights_in, setup, vset, aset, zeroed = sem("weights_in"), sem("setup"), sem("vset"), sem("aset"), sem("zeroed")
        ct_in = [sem(f"ct_in{s}") for s in range(2)]
        x_in = [sem(f"x_in{s}") for s in range(2)]
        xr_in = [sem(f"xr_in{s}") for s in range(2)]
        kout = [sem(f"kout{s}") for s in range(2)]
        qout = [sem(f"qout{s}") for s in range(2)]
        kst_in = [sem(f"kst_in{s}") for s in range(2)]
        xr_done = sem("xr_done")
        mout = [sem(f"mout{s}") for s in range(2)]
        mst_in = [sem(f"mst_in{s}") for s in range(2)]
        x1_out = [sem(f"x1_out{s}") for s in range(2)]
        meta_out = [sem(f"meta_out{s}") for s in range(2)]
        scat = [sem(f"scat{s}") for s in range(2)]
        stat_a, rstd_a, xn_a = sem("stat_a"), sem("rstd_a"), sem("xn_a")
        xt_ps, xnT_a, q_ps, q_hi, q_rest, q_done = (sem(n) for n in ("xt_ps", "xnT_a", "q_ps", "q_hi", "q_rest", "q_done"))
        k_ps, k_hi, k_rest, k_done = (sem(n) for n in ("k_ps", "k_hi", "k_rest", "k_done"))
        v_ps, v_done = sem("v_ps"), sem("v_done")
        s_ps, s_max, max_ps, m_taken, m_done = sem("s_ps"), sem("s_max"), sem("max_ps"), sem("m_taken"), sem("m_done")
        e_ps, e_done = sem("e_ps"), sem("e_done")
        o_ps, o_done, oT_ps, oT_done, y_ps, x1_done = (sem(n) for n in ("o_ps", "o_done", "oT_ps", "oT_done", "y_ps", "x1_done"))
        stat_d, rstd_d, xn_d, x2T_ps, x2T_done = (sem(n) for n in ("stat_d", "rstd_d", "xn_d", "x2T_ps", "x2T_done"))
        lg_ps, lg_done, cnt_done, pos_ps, pos_done, gx_in, ex_done, meta_done, sent_done = (
            sem(n) for n in ("lg_ps", "lg_done", "cnt_done", "pos_ps", "pos_done", "gx_in", "ex_done", "meta_done", "sent_done"))
        vchain, achain, gchain = sem("vchain"), sem("achain"), sem("gchain")
        spass, gpass = sem("spass"), sem("gpass")
        PEEL, PERIOD, BEATS = 8, 4, H
        K_BEATS, V_BEATS, O_BEATS = (4, 5), (7, 10, 13), (3, 14)
        HEADS = [range(max(0, k - O_BEATS[0]) * H // (O_BEATS[1] - O_BEATS[0]), max(0, k + 1 - O_BEATS[0]) * H // (O_BEATS[1] - O_BEATS[0])) if k < O_BEATS[1] else range(0)
                 for k in range(BEATS)]
        EXPS = [range(k * 12 // BEATS, (k + 1) * 12 // BEATS) for k in range(BEATS)]
        block = work.enter_context(nc.Block())

        @block.sync
        def _(sp):
            for dst, src in ((wq_s, wq), (wk_s, wk), (wv_s, wv), (wp_s, wp), (wg_s, wg)):
                sp.dma_start(dst[:, :, :], src.rearrange("(h p) n -> p h n", p=128)).then_inc(weights_in, 16)
            sp.dma_start(cst[:, :], consts).then_inc(weights_in, 16)
            sp.dma_start(gain[:, :], gates).then_inc(weights_in, 16)
            sp.dma_start(bias[:, :], bp).then_inc(weights_in, 16)

            def need(signal, value):
                if not (isinstance(value, int) and value <= 0):
                    hold(sp, signal, value, spass)

            def step(load, proj, minus, out, route):
                if minus:
                    b, s, r = minus.b, minus.slot(2), minus.round(2)
                    need(m_done, b + 1)
                    need(mst_in[s], 16 * r)
                    sp.dma_start(mstage_d[s], mpart[:, s].rearrange("h a t -> h (a t)")).then_inc(mout[s], 16)
                if load:
                    b, s, r = load.b, load.slot(2), load.round(2)
                    need(xn_a, b - 1)
                    sp.dma_start(xt[:, s, :], at(x, b)).then_inc(x_in[s], 16)
                if out:
                    b, s, r = out.b, out.slot(2), out.round(2)
                    need(x1_done, b - 1)
                    sp.dma_start(xr[:, s, :], at(x, b)).then_inc(xr_in[s], 16)
                if minus:
                    b, s, r = minus.b, minus.slot(2), minus.round(2)
                    need(mout[s], 16 * (r + 1))
                    sp.dma_start(qst[STACK:NST, minus.slot(4), :, :], mstage_d[s].rearrange("h (a t) -> a h t", a=3)).then_inc(mst_in[s], 16)
                if proj:
                    b, s, r = proj.b, proj.slot(2), proj.round(2)
                    need(q_done, b + 1)
                    need(kst_in[s], r * 192)
                    sp.dma_start(qstage_d[s].rearrange("(n p) f -> p n f", p=128), qpart[:, s].rearrange("p a h m -> p (a h) m")).then_inc(qout[s], 16)
                    need(k_done, b + 1)
                    sp.dma_start(kstage_d[s].rearrange("(n p) f -> p n f", p=128), kpart[:, s].rearrange("p a h m -> p (a h) m")).then_inc(kout[s], 16)
                    need(e_ps, (b - 3) * 12)
                    kv = kstage_d[s].rearrange("(a h d) f -> a d h f", d=HD, a=3)
                    qv = qstage_d[s].rearrange("(a h d) f -> a d h f", d=HD, a=3)
                    need(qout[s], 16 * (r + 1))
                    for n, (qp, kp) in enumerate(PAIRS):
                        sp.dma_start(qst[n * HD:(n + 1) * HD, proj.slot(4), :, :], qv[qp]).then_inc(kst_in[s], 16)
                    need(kout[s], 16 * (r + 1))
                    for n, (qp, kp) in enumerate(PAIRS):
                        sp.dma_start(kst[n * HD:(n + 1) * HD, proj.slot(4), :, :], kv[kp]).then_inc(kst_in[s], 16)
                if load:
                    b, s, r = load.b, load.slot(2), load.round(2)
                    need(v_ps, (b - 1) * 2)
                    sp.dma_start(ct[:, s, :, :], ctxT[bass.ds(b, 1), :, :].rearrange("a (h p) m -> p (a h) m", p=128)).then_inc(ct_in[s], 16)
                if route:
                    b, s, r = route.b, route.slot(2), route.round(2)
                    need(x1_done, b + 1)
                    sp.dma_start(at(x1_d, b), x1[:, s, :]).then_inc(x1_out[s], 16)
                    need(meta_done, b + 1)
                    sp.dma_start(at(slot_d, b), fetch[:, s, :]).then_inc(meta_out[s], 16)
                    sp.dma_start(at(gate_d, b), gt[:, s, :]).then_inc(meta_out[s], 16)

            pipeline(sp, B, (0, 2, 4, 6, 7), PEEL, step, PERIOD)
            for s in range(2):
                sp.wait_ge(x1_out[s], 16 * (B // 2))
                sp.wait_ge(meta_out[s], 32 * (B // 2))

        @block.gpsimd
        def _(pool):
            chain = Chain(pool, gchain)
            chain.done(pool.memset(eps[:, :], LN_EPS))
            chain.done(pool.memset(zeros[:, :], 0.0))
            chain.done(pool.memset(kst[96:NST, :, :, :], 1.0))
            chain.done(pool.memset(vt[:, :, :, :, HD:HD + 1], 1.0))
            chain.done(pool.memset(total[:, :], 0.0))
            pool.sem_inc(setup, 1)
            every = disp_d.rearrange("(p n a) d -> n p (a d)", p=T, n=8)
            for n in range(8):
                pool.dma_start(every[n], zeros[:, :]).then_inc(zeroed, 16)
            pool.wait_ge(zeroed, 128)

            def split(b, s, part, rest, taken, given):
                hold(pool, taken, b, gpass)
                chain.restart()
                chain.done(pool.tensor_copy(part[:, s, 1], rest[:, s]))
                pool.tensor_tensor(part[:, s, 2], rest[:, s], part[:, s, 1], ALU.subtract).then_inc(given, 1)

            def step(proj, out, route):
                if proj:
                    b, s, r = proj.b, proj.slot(2), proj.round(2)
                    split(b + 1, s, qpart, qrest, q_rest, q_done)
                    split((b + 1) * 2, s, kpart, krest, k_rest, k_done)
                if out:
                    b, s, r = out.b, out.slot(2), out.round(2)
                    hold(pool, xr_in[s], 16 * (r + 1), gpass)
                    pool.tensor_tensor(xr[:, s, :], xr[:, s, :], bias[:, :], ALU.add).then_inc(xr_done, 1)
                if route:
                    b, s, r = route.b, route.slot(2), route.round(2)
                    hold(pool, sent_done, b + 1, gpass)
                    for k in range(2):
                        pool.indirect_dma_start(disp_d, bass.IndirectOffsetOnAxis(ap=sent[:, s, k:k + 1], axis=0),
                                                xn2[:, s, :], None, bounds_check=E * CAP - 1, oob_is_err=False).then_inc(scat[s], 16)

            pool.wait_ge(vset, 1)
            pipeline(pool, B, (1, 5, 6), PEEL, step, PERIOD)
            for s in range(2):
                pool.wait_ge(scat[s], 32 * (B // 2))

        @block.scalar
        def _(act):
            chain = Chain(act, achain)
            act.wait_ge(weights_in, 128)
            act.wait_ge(setup, 1)
            act.activation(tg[:, :], gain[:, :], ACT.Tanh).then_inc(aset, 1)
            act.preload_act_table_set("natural_log_exp_and_others")

            def inverse_root(taken, value, var, log, out, given):
                chain.restart()
                act.wait_ge(taken, value)
                chain.done(act.activation(log, var, ACT.Ln, bias=eps[:, 0:1]))
                act.activation(out, log, ACT.Exp, scale=-0.5).then_inc(given, 1)

            def step(norm, proj, score, out, route):
                for k in range(BEATS):
                    if score:
                        b, s, r = score.b, score.slot(2), score.round(2)
                        for u in EXPS[k]:
                            act.wait_ge(e_ps, b * 12 + u + 1)
                            if u == 0:
                                free(act, o_ps, b - 1)
                            t, g = u // 4, u % 4
                            act.activation(probs[:, s, t, g * 4 * T:(g + 1) * 4 * T], pE[u % 2][0:KP, 0:4 * T], ACT.Exp,
                                           scale=SCALE0).then_inc(e_done, 1)
                    if norm and k == 2:
                        s = norm.slot(2)
                        inverse_root(stat_a, norm.b + 1, mv[:, s, 1:2], lnv[:, s:s + 1], rstd[:, s:s + 1], rstd_a)
                    if proj and k == 4:
                        b, s, r = proj.b, proj.slot(2), proj.round(2)
                        act.wait_ge(q_ps, b + 1)
                        free(act, qout[s], 16 * r)
                        act.copy(qpart[:, s, 0].rearrange("p h t -> p (h t)"), pQ).then_inc(q_hi, 1)
                    if proj and k - 1 in K_BEATS:
                        b, s, r, m = proj.b, proj.slot(2), proj.round(2), K_BEATS.index(k - 1)
                        act.wait_ge(k_ps, b * 2 + m + 1)
                        free(act, kout[s], 16 * r)
                        act.copy(kpart[:, s, 0, m], pKV[m][:, 0:M]).then_inc(k_hi, 1)
                    if route and k == 7:
                        act.wait_ge(x2T_ps, route.b + 1)
                        act.copy(xn2T[:, :, :].rearrange("p h t -> p (h t)"), pT).then_inc(x2T_done, 1)
                    if proj and k in (14, 15):
                        b, s, r, n = proj.b, proj.slot(4), proj.round(2), k - 14
                        lo, hi = ((0, 2), (2, 3))[n]
                        act.wait_ge(v_ps, b * 2 + n + 1)
                        free(act, o_ps, b - 3)
                        act.copy(vt[:, s, lo:hi, :, 0:HD],
                                 pKV[n][0:KP, 0:(hi - lo) * D].rearrange("p (t h d) -> p t h d", t=hi - lo, h=H)).then_inc(v_done, 1)
                    if route and k == 0:
                        act.wait_ge(oT_ps, route.b + 1)
                        act.copy(oT[:, :, :].rearrange("p h t -> p (h t)"), pO[:, 0:DH * T]).then_inc(oT_done, 1)
                    if route and k == 10:
                        act.wait_ge(gx_in, route.b + 1)
                        act.activation(gx[:, 1:2], gx[:, 0:1], ACT.Exp).then_inc(ex_done, 1)
                    if route and k == 3:
                        inverse_root(stat_d, route.b + 1, mv2[:, 1:2], lnv2[:, :], rstd2[:, :], rstd_d)

            pipeline(act, B, (0, 1, 4, 5, 6), PEEL, step, PERIOD)

        @block.vector
        def _(v):
            chain = Chain(v, vchain)
            v.wait_ge(aset, 1)
            chain.done(v.tensor_scalar(bias[:, :], bias[:, :], tg[:, 0:1], None, ALU.mult))
            v.sem_inc(vset, 1)

            def moments(x_in_sem, value, rows, st, out, given):
                chain.restart()
                v.wait_ge(x_in_sem, value)
                chain.done(v.bn_stats(st, rows))
                v.bn_aggr(out, st).then_inc(given, 1)

            def step(norm, proj, top, minus, out, route):
                for k in range(BEATS):
                    if top:
                        v.wait_ge(s_ps, top.b * H + k + 1)
                        v.reduce_max(mx[:, top.slot(2), k:k + 1], pS[k % 2][0:T, 0:M], axis=X_AXIS).then_inc(s_max, 1)
                    if minus and k == 0:
                        b, s, r = minus.b, minus.slot(2), minus.round(2)
                        chain.restart()
                        v.wait_ge(max_ps, b + 1)
                        v.tensor_scalar(mneg[:, :], pT[0:H, 0:T], -1.0, None, ALU.mult).then_inc(m_taken, 1)
                        v.wait_ge(m_taken, b + 1)
                        free(v, mout[s], 16 * r)
                        chain.done(v.tensor_copy(mpart[:, s, 0], mneg[:, :]))
                        chain.done(v.tensor_tensor(mrest[:, :], mneg[:, :], mpart[:, s, 0], ALU.subtract))
                        chain.done(v.tensor_copy(mpart[:, s, 1], mrest[:, :]))
                        v.tensor_tensor(mpart[:, s, 2], mrest[:, :], mpart[:, s, 1], ALU.subtract).then_inc(m_done, 1)
                    if norm and k == 0:
                        b, s, r = norm.b, norm.slot(2), norm.round(2)
                        moments(x_in[s], 16 * (r + 1), xt[:, s, :], stats[:, :], mv[:, s], stat_a)
                    if route and k == 4:
                        b, s, r = route.b, route.slot(2), route.round(2)
                        v.wait_ge(rstd_d, b + 1)
                        free(v, scat[s], 32 * r)
                        v.tensor_scalar(xn2[:, s, :], x1[:, s, :], mv2[:, 0:1], rstd2[:, :], ALU.subtract, ALU.mult).then_inc(xn_d, 1)
                    if proj and k == 2:
                        b, s, r = proj.b, proj.slot(2), proj.round(2)
                        v.wait_ge(xt_ps, b + 1)
                        v.tensor_copy(xnT[:, s].rearrange("p h t -> p (h t)"), pT).then_inc(xnT_a, 1)
                    if route and k == 2:
                        b, s, r = route.b, route.slot(2), route.round(2)
                        v.wait_ge(xr_done, b + 1)
                        free(v, x1_out[s], 16 * r)
                        v.wait_ge(y_ps, b + 1)
                        v.scalar_tensor_tensor(x1[:, s, :], pO[0:T, 0:D], tg[:, 0:1], xr[:, s, :], ALU.mult, ALU.add).then_inc(x1_done, 1)
                        moments(x1_done, b + 1, x1[:, s, :], st2[:, :], mv2[:, :], stat_d)
                    if proj and k == 5:
                        b, s, r = proj.b, proj.slot(2), proj.round(2)
                        v.wait_ge(q_hi, b + 1)
                        free(v, q_done, b - 1)
                        v.tensor_tensor(qrest[:, s].rearrange("p h t -> p (h t)"), pQ, qpart[:, s, 0].rearrange("p h t -> p (h t)"),
                                        ALU.subtract).then_inc(q_rest, 1)
                    if proj and k - 2 in K_BEATS:
                        b, s, r, m = proj.b, proj.slot(2), proj.round(2), K_BEATS.index(k - 2)
                        v.wait_ge(k_hi, b * 2 + m + 1)
                        free(v, k_done, b - 1)
                        v.tensor_tensor(krest[:, s, m], pKV[m][:, 0:M], kpart[:, s, 0, m], ALU.subtract).then_inc(k_rest, 1)
                    if norm and k == 4:
                        b, s, r = norm.b, norm.slot(2), norm.round(2)
                        v.wait_ge(rstd_a, b + 1)
                        v.tensor_scalar(xn[:, s, :], xt[:, s, :], mv[:, s, 0:1], rstd[:, s:s + 1], ALU.subtract, ALU.mult).then_inc(xn_a, 1)
                    if out and k == O_BEATS[1]:
                        b, s, r = out.b, out.slot(2), out.round(2)
                        pv = pO[0:T, 0:H * (HD + 1)].rearrange("p (h d) -> p h d", h=H)
                        chain.restart()
                        v.wait_ge(o_ps, b + 1)
                        chain.done(v.reciprocal(den[:, :], pv[:, :, HD]))
                        v.tensor_tensor(o[:, :, :], pv[:, :, 0:HD], den[:, :].unsqueeze(2).broadcast_to((T, H, HD)), ALU.mult).then_inc(o_done, 1)
                    if route and k == 9:
                        b, s, r = route.b, route.slot(2), route.round(2)
                        chain.restart()
                        v.wait_ge(lg_ps, b + 1)
                        chain.done(v.tensor_copy(lg[:, :], pR))
                        chain.done(v.max(best[:, :], lg[:, :]))
                        chain.done(v.max_index(topi[:, :], best[:, :], lg[:, :]))
                        v.tensor_tensor(gx[:, 0:1], best[:, 1:2], best[:, 0:1], ALU.subtract).then_inc(gx_in, 1)
                        chain.done(v.tensor_copy(topf[:, 0:2], topi[:, 0:2]))
                        for k2 in range(2):
                            chain.done(v.tensor_scalar(hot[:, k2, :], iota[0:T, 0:E], topf[:, k2:k2 + 1], None, ALU.is_equal))
                        v.tensor_tensor(cnt[:, :], hot[:, 0, :], hot[:, 1, :], ALU.add).then_inc(cnt_done, 1)
                    if route and k == 12:
                        b, s, r = route.b, route.slot(2), route.round(2)
                        chain.restart()
                        v.wait_ge(pos_ps, b + 1)
                        v.tensor_tensor(pos[:, :, :], hot[:, :, :], pR.unsqueeze(1).broadcast_to((T, 2, E)), ALU.mult).then_inc(pos_done, 1)
                        v.wait_ge(pos_done, b + 1)
                        chain.done(v.reduce_sum(pos2[:, :], pos[:, :, :], axis=X_AXIS))
                        chain.done(v.tensor_scalar(over[:, :], pos2[:, :], float(CAP), None, ALU.is_ge))
                        chain.done(v.tensor_scalar(pos2[:, :], pos2[:, :], float(CAP - 1), None, ALU.min))
                        chain.done(v.scalar_tensor_tensor(slotf[:, :], topf[:, 0:2], float(CAP), pos2[:, :], ALU.mult, ALU.add))
                        free(v, meta_out[s], 32 * r)
                        chain.done(v.tensor_copy(fetch[:, s, :], slotf[:, :]))
                        chain.done(v.scalar_tensor_tensor(slotf[:, :], over[:, :], float(1 << 20), slotf[:, :], ALU.mult, ALU.add))
                        free(v, scat[s], 32 * r)
                        v.tensor_copy(sent[:, s, :], slotf[:, :]).then_inc(sent_done, 1)
                        chain.done(v.tensor_tensor(total[:, :], total[:, :], cnt[:, :], ALU.add))
                    if route and k == 13:
                        s = route.slot(2)
                        v.wait_ge(ex_done, route.b + 1)
                        chain.done(v.tensor_scalar(gx[:, 0:1], gx[:, 1:2], 1.0, None, ALU.add))
                        chain.done(v.reciprocal(gt[:, s, 0:1], gx[:, 0:1]))
                        chain.done(v.tensor_tensor(gt[:, s, 1:2], gt[:, s, 0:1], gx[:, 1:2], ALU.mult))
                        chain.done(v.tensor_scalar(over[:, :], over[:, :], -1.0, 1.0, ALU.mult, ALU.add))
                        v.tensor_tensor(gt[:, s, :], gt[:, s, :], over[:, :], ALU.mult).then_inc(meta_done, 1)

            pipeline(v, B, (0, 1, 2, 3, 5, 6), PEEL, step, PERIOD)

        @block.tensor
        def _(pe):
            pe.wait_ge(weights_in, 128)
            pe.wait_ge(setup, 1)

            def step(proj, top, minus, score, out, route):
                def attended(heads):
                    if out and heads:
                        b, s = out.b, out.slot(2)
                        if 0 in heads:
                            pe.wait_ge(e_done, (b + 1) * 12)
                            free(pe, x1_done, b)
                        for h in heads:
                            for t in range(KT):
                                mm = pe.matmul(pO[0:T, h * (HD + 1):(h + 1) * (HD + 1)], probs[:, s, t, h * T:(h + 1) * T], vt[:, out.slot(4), t, h, :],
                                               start=t == 0, stop=t == KT - 1)
                        if H - 1 in heads:
                            mm.then_inc(o_ps, 1)

                for k in range(BEATS):
                    if top:
                        b, s, r = top.b, top.slot(2), top.round(2)
                        if k == 0:
                            pe.wait_ge(kst_in[s], 192 * (r + 1))
                        free(pe, s_max, b * H + k - 1)
                        pe.matmul(pS[k % 2][0:T, 0:M], qst[0:STACK, top.slot(4), k, :], kst[0:STACK, top.slot(4), k, :], start=True, stop=True).then_inc(s_ps, 1)
                    if score:
                        b, s, r = score.b, score.slot(4), score.round(2)
                        for u in EXPS[k]:
                            if u == 0:
                                pe.wait_ge(mst_in[score.slot(2)], 16 * (r + 1))
                            t, g = u // 4, u % 4
                            free(pe, e_done, b * 12 + u - 1)
                            for h in range(4):
                                mm = pe.matmul(pE[u % 2][0:KP, h * T:(h + 1) * T], kst[:, s, g * 4 + h, t * KP:(t + 1) * KP],
                                               qst[:, s, g * 4 + h, :], start=True, stop=True)
                            mm.then_inc(e_ps, 1)
                    if minus and k == 0:
                        b = minus.b
                        pe.wait_ge(s_max, (b + 1) * H)
                        free(pe, q_rest, upto(b + 2, B))
                        free(pe, pos_done, b - 3)
                        pe.transpose(pT[0:H, 0:T], mx[:, minus.slot(2), :], ident[0:T, 0:T]).then_inc(max_ps, 1)
                    if proj and k == 1:
                        b, s, r = proj.b, proj.slot(2), proj.round(2)
                        pe.wait_ge(xn_a, b + 1)
                        free(pe, q_rest, b)
                        free(pe, m_taken, b - 1)
                        free(pe, pos_done, b - 5)
                        for h in range(DH):
                            mm = pe.transpose(pT[:, h * T:(h + 1) * T], xn[:, s, h * 128:(h + 1) * 128], ident[0:T, 0:T])
                        mm.then_inc(xt_ps, 1)
                    attended(HEADS[k])
                    if proj and k == 3:
                        b, s, r = proj.b, proj.slot(2), proj.round(2)
                        pe.wait_ge(xnT_a, b + 1)
                        for m in range(DH):
                            for h in range(DH):
                                mm = pe.matmul(pQ[:, m * T:(m + 1) * T], wq_s[:, h, m * 128:(m + 1) * 128], xnT[:, s, h, :],
                                               start=h == 0, stop=h == DH - 1)
                        mm.then_inc(q_ps, 1)
                    if proj and k in K_BEATS:
                        b, s, r, m = proj.b, proj.slot(2), proj.round(2), K_BEATS.index(k)
                        if m == 0:
                            pe.wait_ge(ct_in[s], 16 * (r + 1))
                            free(pe, v_done, b * 2)
                        for h in range(DH):
                            mm = pe.matmul(pKV[m][:, 0:M], wk_s[:, h, m * 128:(m + 1) * 128], ct[:, s, h, :], start=h == 0, stop=h == DH - 1)
                        mm.then_inc(k_ps, 1)
                    if route and k == 6:
                        b, s, r = route.b, route.slot(2), route.round(2)
                        pe.wait_ge(xn_d, b + 1)
                        pe.wait_ge(q_rest, upto(b + 6, B))
                        pe.wait_ge(m_taken, upto(b + 4, B))
                        for h in range(DH):
                            mm = pe.transpose(pT[:, h * T:(h + 1) * T], xn2[:, s, h * 128:(h + 1) * 128], ident[0:T, 0:T])
                        mm.then_inc(x2T_ps, 1)
                    if proj and k in V_BEATS:
                        b, s, t = proj.b, proj.slot(2), V_BEATS.index(k)
                        if t != 1:
                            pe.wait_ge(k_rest, b * 2 + t // 2 + 1)
                        for h in range(DH):
                            mm = pe.matmul(pKV[t // 2][0:KP, (t % 2) * D:(t % 2 + 1) * D], ct[:, s, h, t * KP:(t + 1) * KP], wv_s[:, h, :],
                                           start=h == 0, stop=h == DH - 1)
                        if t != 0:
                            mm.then_inc(v_ps, 1)
                    if route and k == 8:
                        pe.wait_ge(x2T_done, route.b + 1)
                        for h in range(DH):
                            mm = pe.matmul(pR, xn2T[:, h, :], wg_s[:, h, :], start=h == 0, stop=h == DH - 1)
                        mm.then_inc(lg_ps, 1)
                    if out and k == 15:
                        pe.wait_ge(o_done, out.b + 1)
                        for h in range(DH):
                            mm = pe.transpose(pO[:, h * T:(h + 1) * T], o[:, h * HPT:(h + 1) * HPT, :].rearrange("p h d -> p (h d)"), ident[0:T, 0:T])
                        mm.then_inc(oT_ps, 1)
                    if route and k == 1:
                        pe.wait_ge(oT_done, route.b + 1)
                        for h in range(DH):
                            mm = pe.matmul(pO[0:T, 0:D], oT[:, h, :], wp_s[:, h, :], start=h == 0, stop=h == DH - 1)
                        mm.then_inc(y_ps, 1)
                    if route and k == 11:
                        pe.wait_ge(cnt_done, route.b + 1)
                        free(pe, meta_done, route.b)
                        pe.matmul(pR, before[0:T, :], cnt[:, :], start=True, stop=False)
                        pe.matmul(pR, ones[0:T, :], total[:, :], start=False, stop=True).then_inc(pos_ps, 1)

            pipeline(pe, B, (1, 2, 3, 4, 5, 6), PEEL, step, PERIOD)

        work.close()
        at_rest(nc, signals)




CH = 224
UNITS = E * CAP // CH
PER = CAP // CH
RT = CH // T
FT = FF // 128


def experts(nc, w1, w2, consts, disp_d, eout_d):
    ctx, work = ExitStack(), ExitStack()
    with ctx:
        def sb(name, shape, dt=F32):
            return ctx.enter_context(nc.sbuf_tensor(name, shape, dt))

        def sem(name):
            signals.append(ctx.enter_context(nc.semaphore(name)))
            return signals[-1]

        signals = []

        ident = sb("ident_b", [128, 128])
        w1_s = sb("w1_s", [128, 2, DH, 2 * FF])
        w2_s = sb("w2_s", [128, 2, FT, D])
        rows = sb("rows", [T, 2, RT, D])
        rowsT = sb("rowsT", [128, 2, DH, CH])
        act_g = sb("act_g", [128, 2, CH])
        hT = sb("hT", [128, 2, FT, CH])
        y = sb("y", [T, 2, RT, D])
        bank = [ctx.enter_context(nc.psum_tensor(f"ebank{i}", [128, 512], F32)) for i in range(8)]
        pT, pH, pY = bank[0:2], bank[2:6], bank[6:8]

        id_in, spass, gpass = sem("id_in"), sem("spass_b"), sem("gpass_b")
        w_in = [sem(f"w_in{s}") for s in range(2)]
        rows_in = [sem(f"rows_in{s}") for s in range(2)]
        y_out = [sem(f"y_out{s}") for s in range(2)]
        t_ps, t_done, h_ps, g_done, h_done, y_ps, y_done = (
            sem(n) for n in ("t_ps", "t_done", "h_ps", "g_done", "h_done", "y_ps_b", "y_done"))
        block = work.enter_context(nc.Block())
        disp_v = disp_d.rearrange("(u t p) d -> u p t d", t=RT, p=T)
        eout_v = eout_d.rearrange("(u t p) d -> u p t d", t=RT, p=T)

        def unit(ap, b):
            return ap[bass.ds(b, 1)].rearrange("a p t d -> p (a t) d")

        @block.sync
        def _(sp):
            def need(signal, value):
                if not (isinstance(value, int) and value <= 0):
                    hold(sp, signal, value, spass)

            sp.dma_start(ident[:, :], consts[:, 0:128]).then_inc(id_in, 16)

            def step(tile):
                b, s = tile.b, tile.slot(2)
                if tile.place % PER == 0:
                    ws = tile.slot(2 * PER) // PER
                    expert = tile.rounds * 2 + ws
                    need(y_ps, b - PER)
                    sp.dma_start(w1_s[:, ws], w1[bass.ds(expert, 1), :, :].rearrange("a (h p) n -> p (a h) n", p=128)).then_inc(w_in[ws], 16)
                    sp.dma_start(w2_s[:, ws], w2[bass.ds(expert, 1), :, :].rearrange("a (h p) n -> p (a h) n", p=128)).then_inc(w_in[ws], 16)
                need(t_ps, b - 1)
                sp.dma_start(rows[:, s], unit(disp_v, b)).then_inc(rows_in[s], 16)

            pipeline(sp, UNITS, (0,), 2 * PER, step, 2 * PER)

        @block.gpsimd
        def _(pool):
            def step(tile):
                hold(pool, y_done, tile.b + 1, gpass)
                s = tile.slot(2)
                pool.dma_start(unit(eout_v, tile.b), y[:, s]).then_inc(y_out[s], 16)

            pipeline(pool, UNITS, (0,), 2 * PER, step, 2 * PER)
            for s in range(2):
                pool.wait_ge(y_out[s], 16 * (UNITS // 2))

        @block.scalar
        def _(act):
            act.preload_act_table(ACT.Gelu)

            def step(up):
                if up:
                    for j in range(FT):
                        act.wait_ge(h_ps, up.b * FT + j + 1)
                        free(act, h_done, up.b * FT + j - 1)
                        act.activation(act_g[:, j % 2, :], pH[j][:, 0:CH], ACT.Gelu).then_inc(g_done, 1)

            pipeline(act, UNITS, (0,), 2 * PER, step, 2 * PER)

        @block.vector
        def _(v):
            def step(turn, up, down):
                if turn:
                    s = turn.slot(2)
                    v.wait_ge(t_ps, turn.b + 1)
                    free(v, h_ps, (turn.b - 1) * FT)
                    v.tensor_copy(rowsT[:, s].rearrange("p h c -> p (h c)"), pT[s][:, 0:DH * CH]).then_inc(t_done, 1)
                if down:
                    s = down.slot(2)
                    v.wait_ge(y_ps, down.b + 1)
                    free(v, y_out[s], 16 * down.round(2))
                    v.tensor_copy(y[:, s].rearrange("p t d -> p (t d)"), pY[s][0:T, :]).then_inc(y_done, 1)
                if up:
                    s = up.slot(2)
                    for j in range(FT):
                        v.wait_ge(g_done, up.b * FT + j + 1)
                        free(v, y_ps, up.b - 1)
                        v.tensor_tensor(hT[:, s, j, :], act_g[:, j % 2, :], pH[j][:, CH:2 * CH], ALU.mult).then_inc(h_done, 1)

            pipeline(v, UNITS, (0, 1, 2), 2 * PER, step, 2 * PER)

        @block.tensor
        def _(pe):
            pe.wait_ge(id_in, 16)

            def step(turn, up, down):
                if turn:
                    s = turn.slot(2)
                    pe.wait_ge(rows_in[s], 16 * (turn.round(2) + 1))
                    free(pe, t_done, turn.b - 1)
                    for h in range(DH):
                        for t in range(RT):
                            mm = pe.transpose(pT[s][:, h * CH + t * T:h * CH + (t + 1) * T], rows[:, s, t, h * 128:(h + 1) * 128], ident[0:T, 0:T])
                    mm.then_inc(t_ps, 1)
                if down:
                    s, ws = down.slot(2), down.place // PER
                    pe.wait_ge(h_done, (down.b + 1) * FT)
                    free(pe, y_done, down.b - 1)
                    for t in range(RT):
                        for j in range(FT):
                            mm = pe.matmul(pY[s][0:T, t * D:(t + 1) * D], hT[:, s, j, t * T:(t + 1) * T], w2_s[:, ws, j, :],
                                           start=j == 0, stop=j == FT - 1)
                    mm.then_inc(y_ps, 1)
                if up:
                    s, ws = up.slot(2), up.place // PER
                    if up.place % PER == 0:
                        pe.wait_ge(w_in[ws], 32 * (up.rounds + 1))
                    pe.wait_ge(t_done, up.b + 1)
                    for j in range(FT):
                        free(pe, h_done, (up.b - 1) * FT + j + 1)
                        for g in range(2):
                            for h in range(DH):
                                col = (g * FT + j) * 128
                                mm = pe.matmul(pH[j][:, g * CH:(g + 1) * CH], w1_s[:, ws, h, col:col + 128], rowsT[:, s, h, :],
                                               start=h == 0, stop=h == DH - 1)
                        mm.then_inc(h_ps, 1)

            pipeline(pe, UNITS, (0, 1, 2), 2 * PER, step, 2 * PER)

        work.close()
        at_rest(nc, signals)




SCALE1 = D ** -0.5


def cross(nc, x1_d, eout_d, slot_d, gate_d, ctxT, ctxN, wqc, wks, wkc, wqs, wvsT, wvcT, wgT, bcols, brows, gates, consts, interp, x2_d, x3_d):
    ctx, work = ExitStack(), ExitStack()
    with ctx:
        def sb(name, shape, dt=F32):
            return ctx.enter_context(nc.sbuf_tensor(name, shape, dt))

        def sem(name):
            signals.append(ctx.enter_context(nc.semaphore(name)))
            return signals[-1]

        signals = []

        cst = sb("cst_c", [128, 512])
        ident = cst[:, 0:128]
        onerow = sb("onerow", [1, 128])
        wraw = sb("wraw", [128, 4, DH, D])
        wvs, wvc = sb("wvs", [128, DH, D]), sb("wvc", [128, DH, D])
        wg = sb("wg_c", [128, 2 * DH, D])
        bc = sb("bc", [128, DH, 4])
        br = sb("br", [T, 3, D])
        gain, tg, eps = sb("gain_c", [T, 4]), sb("tg_c", [T, 4]), sb("eps_c", [T, 1])
        win = sb("win", [KP, KT, T])
        g1, g2 = sb("g1", [128, DH, D]), sb("g2", [128, DH, D])
        g1b, g2b, w2 = sb("g1b", [128, DH]), sb("g2b", [128, DH]), sb("w2", [128, DH])
        bb = sb("bb", [1, 1])
        x1 = sb("x1_c", [T, 2, D])
        slots = sb("slots", [T, 2, 2], I32)
        gt = sb("gt_c", [T, 2, 2])
        wt = sb("wt", [T, 2])
        er = sb("er", [T, 2, 2, D])
        x2 = sb("x2", [T, 4, D])
        st, mv, lnv, rstd = sb("st_c", [T, 6]), sb("mv_c", [T, 2]), sb("lnv_c", [T, 1]), sb("rstd_c", [T, 1])
        xn, xnT = sb("xn_c", [T, D]), sb("xnT_c", [128, DH, T])
        aT = sb("aT", [128, 2, 2, DH, T])
        vc = sb("vc", [T, 4, D])
        dr = sb("dr", [1, 2, T])
        ct = sb("ct_c", [128, 2, DH, M])
        cn = sb("cn", [KP, 4, KT, D])
        m1, n1, l1, r1 = sb("m1", [T, 1]), sb("n1", [T, 1]), sb("l1", [T, 1]), sb("r1", [T, 2])
        m2, n2, l2, r2 = sb("m2", [KP, KT]), sb("n2", [KP, KT]), sb("l2", [KP, KT]), sb("r2", [KP, KT])
        p1, p1T = sb("p1", [T, M]), sb("p1T", [KP, 2, KT, T])
        p2, p2n = sb("p2", [KP, KT, T]), sb("p2n", [KP, 2, KT, T])
        c1T, p2iT = sb("c1T", [128, DH, T]), sb("p2iT", [T, T])
        both = sb("both", [T, 2, 2, D])
        bT = sb("bT", [128, 2 * DH, T])
        gl, ge, gr, df = sb("gl", [T, D]), sb("ge", [T, D]), sb("gr", [T, D]), sb("df", [T, D])
        x3 = sb("x3", [T, 2, D])

        bank = [ctx.enter_context(nc.psum_tensor(f"cbank{i}", [128, 512], F32)) for i in range(8)]
        bX, bA, bV, bS1, bS2, bR, bC, bG = bank

        w_in, setup, vset, spass, gpass, vpass = (sem(n) for n in ("w_in_c", "setup_c", "vset_c", "spass_c", "gpass_c", "vpass_c"))
        wset_ps = sem("wset_ps")
        x1_in = [sem(f"x1_in{s}") for s in range(2)]
        meta_in = [sem(f"meta_in{s}") for s in range(2)]
        er_in = [sem(f"er_in{s}") for s in range(2)]
        ct_in = [sem(f"ct_in_c{s}") for s in range(2)]
        cn_in = [sem(f"cn_in{s}") for s in range(4)]
        x3_out = [sem(f"x3_out{s}") for s in range(2)]
        (x2_done, stat_done, rstd_done, xn_done, xt_ps, xnT_done, a_ps, a_done, v_ps, v_done,
         s1_ps, s2_ps, n1_done, n2_done, e1_done, e2_done, t1_ps, t1_done, p2_done,
         c_ps, c_done, y_ps, y_done, gt_ps, gt_done, g_ps, gl_done, ge_done, x3_done) = (sem(n + "_c") for n in (
             "x2_done stat_done rstd_done xn_done xt_ps xnT_done a_ps a_done v_ps v_done "
             "s1_ps s2_ps n1_done n2_done e1_done e2_done t1_ps t1_done p2_done "
             "c_ps c_done y_ps y_done gt_ps gt_done g_ps gl_done ge_done x3_done").split())
        vchain, achain = sem("vchain_c"), sem("achain_c")
        block = work.enter_context(nc.Block())
        PERIOD, PEEL = 4, 8

        @block.sync
        def _(sp):
            def need(signal, value):
                if not (isinstance(value, int) and value <= 0):
                    hold(sp, signal, value, spass)

            for n, w in enumerate((wqc, wks, wkc, wqs)):
                sp.dma_start(wraw[:, n], w.rearrange("(h p) n -> p h n", p=128)).then_inc(w_in, 16)
            for dst, w in ((wvs, wvsT), (wvc, wvcT), (wg, wgT), (bc, bcols)):
                sp.dma_start(dst[:, :, :], w.rearrange("(h p) n -> p h n", p=128)).then_inc(w_in, 16)
            sp.dma_start(br[:, :, :], brows).then_inc(w_in, 16)
            sp.dma_start(gain[:, :], gates).then_inc(w_in, 16)
            sp.dma_start(cst[:, :], consts).then_inc(w_in, 16)
            sp.dma_start(win[:, :, :], interp).then_inc(w_in, 16)

            def step(load, ctxs, out):
                if load:
                    b, s = load.b, load.slot(2)
                    need(er_in[s], 32 * load.round(2))
                    need(x2_done, b - 1)
                    sp.dma_start(slots[:, s, :], at(slot_d, b)).then_inc(meta_in[s], 16)
                    sp.dma_start(gt[:, s, :], at(gate_d, b)).then_inc(meta_in[s], 16)
                    sp.dma_start(x1[:, s, :], at(x1_d, b)).then_inc(x1_in[s], 16)
                if ctxs:
                    b, s = ctxs.b, ctxs.slot(2)
                    need(s2_ps, b - 1)
                    sp.dma_start(ct[:, s], ctxT[bass.ds(b, 1), :, :].rearrange("a (h p) m -> p (a h) m", p=128)).then_inc(ct_in[s], 16)
                    need(c_ps, b - 3)
                    sp.dma_start(cn[:, ctxs.slot(4)], ctxN[bass.ds(b, 1), :, :].rearrange("a (t p) d -> p (a t) d", p=KP)).then_inc(cn_in[ctxs.slot(4)], 16)
                if out:
                    b, s = out.b, out.slot(2)
                    need(x3_done, b + 1)
                    sp.dma_start(at(x3_d, b), x3[:, s, :]).then_inc(x3_out[s], 16)

            pipeline(sp, B, (0, 1, 5), PEEL, step, PERIOD)
            for s in range(2):
                sp.wait_ge(x3_out[s], 16 * (B // 2))

        @block.gpsimd
        def _(pool):
            pool.memset(eps[:, :], LN_EPS).then_inc(setup, 1)
            pool.wait_ge(setup, 1)
            pool.memset(onerow[:, :], 1.0).then_inc(setup, 1)

            def step(load):
                b, s = load.b, load.slot(2)
                hold(pool, meta_in[s], 32 * (load.round(2) + 1), gpass)
                if not (isinstance(b, int) and b < 2):
                    hold(pool, x2_done, b - 1, gpass)
                for k in range(2):
                    pool.indirect_dma_start(er[:, s, k, :], None, eout_d, bass.IndirectOffsetOnAxis(ap=slots[:, s, k:k + 1], axis=0),
                                            bounds_check=E * CAP - 1, oob_is_err=False).then_inc(er_in[s], 16)

            pipeline(pool, B, (0,), PEEL, step, PERIOD)

        @block.scalar
        def _(act):
            chain = Chain(act, achain)
            act.wait_ge(w_in, 192)
            act.wait_ge(setup, 2)
            act.activation(tg[:, :], gain[:, :], ACT.Tanh).then_inc(vset, 1)
            act.preload_act_table_set("natural_log_exp_and_others")

            def step(p, q, r, z):
                if p:
                    chain.restart()
                    act.wait_ge(stat_done, p.b + 1)
                    chain.done(act.activation(lnv[:, :], mv[:, 1:2], ACT.Ln, bias=eps[:, 0:1]))
                    act.activation(rstd[:, :], lnv[:, :], ACT.Exp, scale=-0.5).then_inc(rstd_done, 1)
                if q:
                    act.wait_ge(n1_done, q.b + 1)
                    act.activation(p1[:, :], bS1[0:T, 0:M], ACT.Exp, bias=n1[:, 0:1], scale=SCALE1, accum_out=l1[:, 0:1]).then_inc(e1_done, 1)
                    act.wait_ge(n2_done, q.b + 1)
                    free(act, p2_done, q.b)
                    for t in range(KT):
                        e = act.activation(p2[:, t, :], bS2[0:KP, t * T:(t + 1) * T], ACT.Exp, bias=n2[:, t:t + 1], scale=SCALE1,
                                           accum_out=l2[:, t:t + 1])
                    e.then_inc(e2_done, 1)
                if z:
                    act.wait_ge(gt_ps, z.b + 1)
                    act.copy(bT[:, :, :].rearrange("p h t -> p (h t)"), bG[:, 0:2 * DH * T]).then_inc(gt_done, 1)
                if p:
                    s = p.slot(2)
                    act.wait_ge(a_ps, p.b + 1)
                    for n, bias in enumerate((g1b, g2b)):
                        for h in range(DH):
                            col = (n * DH + h) * T
                            e = act.activation(aT[:, s, n, h, :], bA[:, col:col + T], ACT.Identity, bias=bias[:, h:h + 1])
                    e.then_inc(a_done, 1)
                if q:
                    act.wait_ge(t1_ps, q.b + 1)
                    act.copy(p1T[:, q.slot(2)].rearrange("p t q -> p (t q)"), bS1[0:KP, 0:KT * T]).then_inc(t1_done, 1)
                if z:
                    act.wait_ge(gl_done, z.b + 1)
                    act.activation(ge[:, :], gl[:, :], ACT.Exp, scale=-1.0).then_inc(ge_done, 1)

            pipeline(act, B, (0, 1, 2, 3), PEEL, step, PERIOD)

        @block.vector
        def _(v):
            chain = Chain(v, vchain)
            v.wait_ge(wset_ps, 1)
            for n, g in enumerate((g1, g2)):
                for h in range(DH):
                    chain.done(v.tensor_copy(g[:, h, :], bank[n][:, h * D:(h + 1) * D]))
            for n, g in enumerate((g1b, g2b, w2)):
                chain.done(v.tensor_copy(g[:, :], bank[2][:, n * DH:(n + 1) * DH]))
            chain.done(v.tensor_copy(bb[:, :], bank[2][0:1, 16:17]))
            v.wait_ge(vset, 1)
            v.sem_inc(vset, 1)

            def step(p, q, r, z):
                if p:
                    b, s = p.b, p.slot(2)
                    chain.restart()
                    v.wait_ge(meta_in[s], 32 * (p.round(2) + 1))
                    chain.done(v.tensor_scalar(wt[:, :], gt[:, s, :], tg[:, 2:3], None, ALU.mult))
                    v.wait_ge(x1_in[s], 16 * (p.round(2) + 1))
                    v.wait_ge(er_in[s], 32 * (p.round(2) + 1))
                    x2b = x2[:, p.slot(4), :]
                    chain.done(v.scalar_tensor_tensor(x2b, er[:, s, 0, :], wt[:, 0:1], x1[:, s, :], ALU.mult, ALU.add))
                    v.scalar_tensor_tensor(x2b, er[:, s, 1, :], wt[:, 1:2], x2b, ALU.mult, ALU.add).then_inc(x2_done, 1)
                    v.wait_ge(x2_done, b + 1)
                    chain.done(v.bn_stats(st[:, :], x2b))
                    v.bn_aggr(mv[:, :], st[:, :]).then_inc(stat_done, 1)
                if q:
                    chain.restart()
                    v.wait_ge(s1_ps, q.b + 1)
                    chain.done(v.reduce_max(m1[:, :], bS1[0:T, 0:M], axis=X_AXIS))
                    v.tensor_scalar(n1[:, :], m1[:, :], -SCALE1, None, ALU.mult).then_inc(n1_done, 1)
                    v.wait_ge(s2_ps, q.b + 1)
                    chain.done(v.reduce_max(m2[:, :], bS2[0:KP, 0:KT * T].rearrange("p (t q) -> p t q", t=KT), axis=X_AXIS))
                    v.tensor_scalar(n2[:, :], m2[:, :], -SCALE1, None, ALU.mult).then_inc(n2_done, 1)
                if p:
                    v.wait_ge(rstd_done, p.b + 1)
                    v.tensor_scalar(xn[:, :], x2[:, p.slot(4), :], mv[:, 0:1], rstd[:, :], ALU.subtract, ALU.mult).then_inc(xn_done, 1)
                if r:
                    chain.restart()
                    v.wait_ge(c_ps, r.b + 1)
                    chain.done(v.tensor_copy(c1T[:, :, :].rearrange("p h t -> p (h t)"), bR[:, 0:DH * T]))
                    v.tensor_copy(p2iT[:, :], bR[0:T, DH * T:(DH + 1) * T]).then_inc(c_done, 1)
                if p:
                    v.wait_ge(xt_ps, p.b + 1)
                    v.tensor_copy(xnT[:, :, :].rearrange("p h t -> p (h t)"), bX[:, 0:DH * T]).then_inc(xnT_done, 1)
                    chain.restart()
                    v.wait_ge(v_ps, p.b + 1)
                    chain.done(v.tensor_scalar(dr[:, p.slot(2), :], bV[0:1, D:D + T], bb[:, :], None, ALU.add))
                    v.tensor_tensor(vc[:, p.slot(4), :], bV[0:T, 0:D], br[:, 1, :], ALU.add).then_inc(v_done, 1)
                if q:
                    s = q.slot(2)
                    chain.restart()
                    v.wait_ge(e1_done, q.b + 1)
                    v.wait_ge(e2_done, q.b + 1)
                    chain.done(v.reciprocal(r1[:, s:s + 1], l1[:, :]))
                    chain.done(v.reciprocal(r2[:, :], l2[:, :]))
                    v.tensor_tensor(p2n[:, s], p2[:, :, :], r2[:, :].unsqueeze(2).broadcast_to((KP, KT, T)), ALU.mult).then_inc(p2_done, 1)
                if r:
                    s = r.slot(2)
                    chain.restart()
                    v.wait_ge(y_ps, r.b + 1)
                    chain.done(v.scalar_tensor_tensor(both[:, s, 0, :], bC[0:T, 0:D], r1[:, s:s + 1], br[:, 0, :], ALU.mult, ALU.add))
                    v.tensor_copy(both[:, s, 1, :], bC[0:T, D:2 * D]).then_inc(y_done, 1)
                if z:
                    s = z.slot(2)
                    c2s, s2c = both[:, s, 0, :], both[:, s, 1, :]
                    chain.restart()
                    v.wait_ge(g_ps, z.b + 1)
                    v.tensor_tensor(gl[:, :], bG[0:T, 0:D], br[:, 2, :], ALU.add).then_inc(gl_done, 1)
                    free(v, x3_done, z.b)
                    chain.done(v.tensor_tensor(df[:, :], c2s, s2c, ALU.subtract))
                    v.wait_ge(ge_done, z.b + 1)
                    chain.done(v.tensor_scalar(gr[:, :], ge[:, :], 1.0, None, ALU.add))
                    chain.done(v.reciprocal(gr[:, :], gr[:, :]))
                    chain.done(v.tensor_tensor(df[:, :], df[:, :], gr[:, :], ALU.mult))
                    chain.done(v.tensor_tensor(df[:, :], df[:, :], s2c, ALU.add))
                    free(v, x3_out[s], 16 * z.round(2))
                    v.scalar_tensor_tensor(x3[:, s, :], df[:, :], tg[:, 1:2], x2[:, z.slot(4), :], ALU.mult, ALU.add).then_inc(x3_done, 1)

            pipeline(v, B, (0, 1, 2, 3), PEEL, step, PERIOD)

        @block.tensor
        def _(pe):
            pe.wait_ge(w_in, 192)
            for n, (left, right) in enumerate(((0, 1), (2, 3))):
                for h in range(DH):
                    for k in range(DH):
                        pe.matmul(bank[n][:, h * D:(h + 1) * D], wraw[:, left, k, h * 128:(h + 1) * 128], wraw[:, right, k, :],
                                  start=k == 0, stop=k == DH - 1)
            for n, (w, c) in enumerate(((1, 0), (3, 2), (2, 3))):
                for h in range(DH):
                    for k in range(DH):
                        pe.matmul(bank[2][:, n * DH + h:n * DH + h + 1], wraw[:, w, k, h * 128:(h + 1) * 128], bc[:, k, c:c + 1],
                                  start=k == 0, stop=k == DH - 1)
            for k in range(DH):
                mm = pe.matmul(bank[2][0:1, 16:17], bc[:, k, 3:4], bc[:, k, 2:3], start=k == 0, stop=k == DH - 1)
            mm.then_inc(wset_ps, 1)
            pe.wait_ge(vset, 2)

            def step(p, q, r, z):
                if q:
                    s = q.slot(2)
                    pe.wait_ge(ct_in[s], 16 * (q.round(2) + 1))
                    pe.wait_ge(a_done, q.b + 1)
                    free(pe, t1_done, q.b)
                    for h in range(DH):
                        mm = pe.matmul(bS1[0:T, 0:M], aT[:, s, 0, h, :], ct[:, s, h, :], start=h == 0, stop=h == DH - 1)
                    mm.then_inc(s1_ps, 1)
                    pe.wait_ge(v_done, q.b + 1)
                    free(pe, e2_done, q.b)
                    for t in range(KT):
                        out = bS2[0:KP, t * T:(t + 1) * T]
                        for h in range(DH):
                            pe.matmul(out, ct[:, s, h, t * KP:(t + 1) * KP], aT[:, s, 1, h, :], start=h == 0, stop=False)
                        mm = pe.matmul(out, onerow[0:1, 0:KP], dr[:, s, :], start=False, stop=True)
                    mm.then_inc(s2_ps, 1)
                if r:
                    s = r.slot(2)
                    pe.wait_ge(t1_done, r.b + 1)
                    pe.wait_ge(p2_done, r.b + 1)
                    pe.wait_ge(cn_in[r.slot(4)], 16 * (r.round(4) + 1))
                    free(pe, c_done, r.b)
                    for h in range(DH):
                        for t in range(KT):
                            pe.matmul(bR[:, h * T:(h + 1) * T], cn[:, r.slot(4), t, h * 128:(h + 1) * 128], p1T[:, s, t, :],
                                      start=t == 0, stop=t == KT - 1)
                    for t in range(KT):
                        mm = pe.matmul(bR[0:T, DH * T:(DH + 1) * T], p2n[:, s, t, :], win[:, t, :], start=t == 0, stop=t == KT - 1)
                    mm.then_inc(c_ps, 1)
                if p:
                    pe.wait_ge(xn_done, p.b + 1)
                    free(pe, xnT_done, p.b)
                    for h in range(DH):
                        mm = pe.transpose(bX[:, h * T:(h + 1) * T], xn[:, h * 128:(h + 1) * 128], ident[0:T, 0:T])
                    mm.then_inc(xt_ps, 1)
                if z:
                    s = z.slot(2)
                    pe.wait_ge(y_done, z.b + 1)
                    free(pe, gl_done, z.b)
                    for n in range(2):
                        for h in range(DH):
                            col = (n * DH + h) * T
                            mm = pe.transpose(bG[:, col:col + T], both[:, s, n, h * 128:(h + 1) * 128], ident[0:T, 0:T])
                    mm.then_inc(gt_ps, 1)
                if p:
                    pe.wait_ge(xnT_done, p.b + 1)
                    free(pe, a_done, p.b)
                    for n, g in enumerate((g1, g2)):
                        for h in range(DH):
                            for k in range(DH):
                                mm = pe.matmul(bA[:, (n * DH + h) * T:(n * DH + h + 1) * T], g[:, k, h * 128:(h + 1) * 128], xnT[:, k, :],
                                               start=k == 0, stop=k == DH - 1)
                    mm.then_inc(a_ps, 1)
                    free(pe, v_done, p.b)
                    for k in range(DH):
                        pe.matmul(bV[0:T, 0:D], xnT[:, k, :], wvc[:, k, :], start=k == 0, stop=k == DH - 1)
                    for k in range(DH):
                        mm = pe.matmul(bV[0:1, D:D + T], w2[:, k:k + 1], xnT[:, k, :], start=k == 0, stop=k == DH - 1)
                    mm.then_inc(v_ps, 1)
                if r:
                    pe.wait_ge(c_done, r.b + 1)
                    free(pe, y_done, r.b)
                    for h in range(DH):
                        pe.matmul(bC[0:T, 0:D], c1T[:, h, :], wvs[:, h, :], start=h == 0, stop=h == DH - 1)
                    pe.matmul(bC[0:T, D:2 * D], p2iT[:, :], vc[:, r.slot(4), :], start=True, stop=True).then_inc(y_ps, 1)
                if q:
                    pe.wait_ge(e1_done, q.b + 1)
                    for t in range(KT):
                        mm = pe.transpose(bS1[0:KP, t * T:(t + 1) * T], p1[:, t * KP:(t + 1) * KP], ident[0:T, 0:T])
                    mm.then_inc(t1_ps, 1)
                if z:
                    pe.wait_ge(gt_done, z.b + 1)
                    for k in range(2 * DH):
                        mm = pe.matmul(bG[0:T, 0:D], bT[:, k, :], wg[:, k, :], start=k == 0, stop=k == 2 * DH - 1)
                    mm.then_inc(g_ps, 1)

            pipeline(pe, B, (0, 1, 2, 3), PEEL, step, PERIOD)

        work.close()
        at_rest(nc, signals)




PH, PK, KEYS, DK = 8, 8, 64, 128
PAIR = B // 2
SETS = PH * 2
NC = KEYS * KEYS // 128
GO = 8
TG, CG = T // GO, NC // GO
RMS_EPS = 1e-6


def retrieve(nc, x3_d, wq, keysT, downT, up, norm, gates, consts, out_d):
    ctx, work = ExitStack(), ExitStack()
    with ctx:
        def sb(name, shape, dt=F32):
            return ctx.enter_context(nc.sbuf_tensor(name, shape, dt))

        def sem(name):
            signals.append(ctx.enter_context(nc.semaphore(name)))
            return signals[-1]

        signals = []

        cst = sb("cst_d", [128, 512])
        ident, iota = cst[:, 0:128], cst[:, 352:480]
        gain, tg, eps = sb("gain_d", [T, 4]), sb("tg_d", [T, 4]), sb("eps_d", [T, 2])
        nw = sb("nw", [T, D])
        dT = sb("dT", [128, DH, NC, 128])
        u_s = sb("u_s", [128, NC, D])
        cw = sb("cw", [128, DH, SETS * KEYS])
        g = sb("g", [128, 2, NC, 2 * T])
        wq_s = g[:, 0, :, :].rearrange("p c t -> p (c t)")[:, 0:SETS * D].rearrange("p (s d) -> p s d", s=SETS)
        ks = g[:, 1, :, :].rearrange("p c t -> p (c t)")[:, 0:SETS * KEYS].rearrange("p (s k) -> p s k", s=SETS)
        xs, xl = sb("xs", [T, 2, 2, D]), sb("xl", [T, 2, D])
        st, mv, lnv, rstd = sb("st_d", [T, 2, 6]), sb("mv_d", [T, 2, 2]), sb("lnv_d", [T, 2]), sb("rstd_d_s", [T, 2])
        rsq, ms, inv = sb("rsq", [T, 2]), sb("ms", [T, 2]), sb("inv", [T, 2])
        oT = sb("oT_d", [128, DH, 2 * T])
        xnT = sb("xnT_d", [128, 2, DH, 2 * T])
        sim = sb("sim", [T, 2, 2, SETS * KEYS])
        val = sb("val", [T, 2 * SETS, 8])
        idx = sb("idx", [T, 2 * SETS, 8], U32)
        idxf = sb("idxf", [T, 2 * SETS, 8])
        cand = sb("cand", [T, 2 * PH, PK * PK])
        best = sb("best", [T, 2 * PH, PK])
        ci = sb("ci", [T, 2 * PH, PK], U32)
        cab = sb("cab", [T, 2, 2 * PH, PK], U32)
        cabf = sb("cabf", [T, 2, 2 * PH, PK])
        eq = sb("eq", [T, 2, 2 * PH, PK, 8])
        ij = sb("ij", [T, 2, 2 * PH * PK])
        kin = sb("kin", [T, 3, 2 * PH * PK])
        ef, ei = sb("ef", [T, 2 * PH * PK]), sb("ei", [T, 2, 2 * PH * PK], I32)
        pc = sb("pc", [128, 2, T])
        rp = sb("rp", [128, T, 3], BF16)
        rrest = sb("rrest", [128, T])
        hotp = sb("hotp", [128, 2, TG, 128], BF16)
        hotc = sb("hotc", [128, 2, TG, NC], BF16)
        hotw = sb("hotw", [128, 2, TG, 3, 2 * NC], BF16)
        y = sb("y_d", [T, 2, 2, D])

        bank = [ctx.enter_context(nc.psum_tensor(f"dbank{i}", [128, 512], F32)) for i in range(4)]
        wbank = [ctx.enter_context(nc.psum_tensor(f"wbank{i}", [128, 2, 512], F32)) for i in range(2)]
        bM, bD, bU = bank[0], bank[1:3], bank[3]

        w_in, setup, vset, cset_ps, cset_done, spass, gpass, vpass = (
            sem(n + "_d") for n in "w_in setup vset cset_ps cset_done spass gpass vpass".split())
        x_in = [sem(f"x_in_d{s}") for s in range(2)]
        xr_in = [sem(f"xr_in_d{s}") for s in range(2)]
        y_out = [sem(f"y_out_d{s}") for s in range(2)]
        (stat_done, xl_done, inv_done, xn_done, xt_ps, xnT_done, sim_ps, sim_done, val_done, best_done, kin_done,
         kt_ps, kt_done, hp_done, hc_done, w_ps, w_done, d_ps, g_done, u_ps, y_done, y_ps, oT_done, oc_done, ij_done) = (sem(n + "_p") for n in (
             "stat_done xl_done inv_done xn_done xt_ps xnT_done sim_ps sim_done val_done best_done kin_done "
             "kt_ps kt_done hp_done hc_done w_ps w_done d_ps g_done u_ps y_done y_ps oT_done oc_done ij_done").split())
        vchain, achain, gchain = sem("vchain_d"), sem("achain_d"), sem("gchain_d")
        block = work.enter_context(nc.Block())
        PEEL = 6
        x3_v = x3_d.rearrange("(u t) p d -> u p t d", t=2)
        out_v = out_d.rearrange("(u t) p d -> u p t d", t=2)

        def pair(ap, b):
            return ap[bass.ds(b, 1)].rearrange("a p t d -> p (a t) d")

        @block.sync
        def _(sp):
            def need(signal, value):
                if not (isinstance(value, int) and value <= 0):
                    hold(sp, signal, value, spass)

            sp.dma_start(cst[:, :], consts).then_inc(w_in, 16)
            sp.dma_start(gain[:, :], gates).then_inc(w_in, 16)
            sp.dma_start(nw[:, :], norm).then_inc(w_in, 16)
            sp.dma_start(wq_s, wq.rearrange("(s p) d -> p s d", p=DK)).then_inc(w_in, 16)
            sp.dma_start(ks, keysT).then_inc(w_in, 16)
            sp.dma_start(dT[:, :, :, :], downT.rearrange("(h p) c e -> p h c e", p=128)).then_inc(w_in, 16)
            sp.dma_start(u_s[:, :, :], up.rearrange("(p c) d -> p c d", p=128)).then_inc(w_in, 16)

            def step(load, out):
                if load:
                    b, s = load.b, load.slot(2)
                    need(xl_done, b - 1)
                    sp.dma_start(xs[:, s], pair(x3_v, b)).then_inc(x_in[s], 16)
                if out:
                    b, s = out.b, out.slot(2)
                    need(y_out[s], 16 * out.round(2))
                    sp.dma_start(y[:, s], pair(x3_v, b)).then_inc(xr_in[s], 16)
                    need(y_done, b + 1)
                    sp.dma_start(pair(out_v, b), y[:, s]).then_inc(y_out[s], 16)

            pipeline(sp, PAIR, (0, 4), PEEL, step)
            for s in range(2):
                sp.wait_ge(y_out[s], 16 * (PAIR // 2))

        @block.gpsimd
        def _(pool):
            chain = Chain(pool, gchain)
            chain.done(pool.memset(eps[:, 0:1], LN_EPS))
            chain.done(pool.memset(eps[:, 1:2], RMS_EPS))
            chain.done(pool.memset(hotw[:, :, :, :, :], 0.0))
            pool.sem_inc(setup, 1)
            pool.wait_ge(w_in, 112)

            def step(k, w):
                for n in range(GO):
                    if w:
                        at_n = w.b * GO + n
                        toks = slice(n * TG, (n + 1) * TG)
                        hold(pool, oc_done, at_n + 1, gpass)
                        if not (isinstance(at_n, int) and at_n < 2):
                            hold(pool, w_ps, at_n - 1, gpass)
                        chain.restart()
                        for t in range(2):
                            rows = slice(t * 64, t * 64 + 64)
                            ins = pool.tensor_tensor(hotw[rows, n % 2, :, :, t * NC:(t + 1) * NC],
                                                     hotc[rows, n % 2].unsqueeze(2).broadcast_to((64, TG, 3, NC)),
                                                     rp[rows, toks, :].unsqueeze(3).broadcast_to((64, TG, 3, NC)), ALU.mult)
                            if t == 0:
                                chain.done(ins)
                        ins.then_inc(hc_done, 1)
                        pool.wait_ge(hc_done, at_n + 1)
                    if k and n == 6:
                        hold(pool, best_done, k.b + 1, gpass)
                        chain.restart()
                        for half in range(2):
                            found = idxf[:, :, :].rearrange("p (s a) k -> p s a k", a=2)[:, :, half, :].unsqueeze(2).broadcast_to((T, 2 * PH, PK, 8))
                            ins = pool.tensor_tensor(eq[:, half], eq[:, half], found, ALU.mult)
                            if half == 0:
                                chain.done(ins)
                        ins.then_inc(ij_done, 1)
                        pool.wait_ge(ij_done, k.b + 1)

            pipeline(pool, PAIR, (1, 2), PEEL, step)

        @block.scalar
        def _(act):
            chain = Chain(act, achain)
            act.wait_ge(w_in, 112)
            act.wait_ge(setup, 1)
            act.activation(tg[:, :], gain[:, :], ACT.Tanh).then_inc(vset, 1)

            def step(p, d, up):
                for n in range(GO):
                    if up and n == GO - 1:
                        act.wait_ge(u_ps, up.b + 1)
                        act.copy(oT[:, :, :].rearrange("p h t -> p (h t)"), bU[:, 0:DH * 2 * T]).then_inc(oT_done, 1)
                    if d:
                        for u in range(2):
                            at_u = (d.b * GO + n) * 2 + u
                            c = n * CG + 2 * u
                            act.wait_ge(d_ps, at_u + 1)
                            act.activation(g[:, d.slot(2), c:c + 2, :].rearrange("p c t -> p (c t)"), bD[u][:, 0:4 * T], ACT.Gelu).then_inc(g_done, 1)
                    if p and n == 0:
                        act.preload_act_table_set("natural_log_exp_and_others")
                        chain.restart()
                        act.wait_ge(stat_done, p.b + 1)
                        chain.done(act.activation(lnv[:, :], mv[:, :, 1], ACT.Ln, bias=eps[:, 0:1]))
                        chain.done(act.activation(rstd[:, :], lnv[:, :], ACT.Exp, scale=-0.5))
                        chain.done(act.activation(rsq[:, :], lnv[:, :], ACT.Exp, scale=-1.0))
                        for t in range(2):
                            chain.done(act.activation(ms[:, t:t + 1], rsq[:, t:t + 1], ACT.Identity, scale=mv[:, t, 1:2]))
                        chain.done(act.activation(ms[:, :], ms[:, :], ACT.Ln, bias=eps[:, 1:2]))
                        act.activation(inv[:, :], ms[:, :], ACT.Exp, scale=-0.5).then_inc(inv_done, 1)
                        act.preload_act_table(ACT.Gelu)
                    if p and n == 2:
                        act.wait_ge(xt_ps, p.b + 1)
                        act.copy(xnT[:, p.slot(2)].rearrange("p h t -> p (h t)"), bM[:, 0:4 * T]).then_inc(xnT_done, 1)
                    if p and 3 <= n < 7:
                        q = n - 3
                        act.wait_ge(sim_ps, p.b * 4 + q + 1)
                        free(act, val_done, p.b - 1)
                        act.copy(sim[:, p.slot(2), q // 2, (q % 2) * 512:(q % 2 + 1) * 512], bM[0:T, 0:512]).then_inc(sim_done, 1)

            pipeline(act, PAIR, (0, 1, 3), PEEL, step)

        @block.vector
        def _(v):
            chain = Chain(v, vchain)
            v.wait_ge(cset_ps, 1)
            for n, src in enumerate((wbank[0][:, 0, :], wbank[0][:, 1, :], wbank[1][:, 0, :], wbank[1][:, 1, :])):
                chain.done(v.tensor_copy(cw[:, n // 2, (n % 2) * 512:(n % 2 + 1) * 512], src))
            v.wait_ge(vset, 1)
            v.sem_inc(cset_done, 1)
            FIRST = [(0, 8), (8, 16), (16, 24), (24, 32)]

            def one_hot(b, n):
                v.wait_ge(kt_done, b + 1)
                free(v, hc_done, b * GO + n - 1)
                v.tensor_tensor(hotc[:, n % 2], iota[:, 0:NC].unsqueeze(1).broadcast_to((128, TG, NC)),
                                pc[:, 1, n * TG:(n + 1) * TG].unsqueeze(2).broadcast_to((128, TG, NC)), ALU.is_equal).then_inc(oc_done, 1)
                free(v, w_ps, b * GO + n - 1)
                v.tensor_tensor(hotp[:, n % 2], iota.unsqueeze(1).broadcast_to((128, TG, 128)),
                                pc[:, 0, n * TG:(n + 1) * TG].unsqueeze(2).broadcast_to((128, TG, 128)), ALU.is_equal).then_inc(hp_done, 1)

            def step(p, k, w, up):
                if p:
                    b, s = p.b, p.slot(2)
                    chain.restart()
                    v.wait_ge(x_in[s], 16 * (p.round(2) + 1))
                    for t in range(2):
                        chain.done(v.bn_stats(st[:, t], xs[:, s, t, :]))
                    chain.done(v.bn_aggr(mv[:, 0], st[:, 0]))
                    v.bn_aggr(mv[:, 1], st[:, 1]).then_inc(stat_done, 1)
                for n in range(GO):
                    if w and n < GO - 1:
                        one_hot(w.b, n + 1)
                    if p and n == 1:
                        s = p.slot(2)
                        chain.restart()
                        v.wait_ge(inv_done, p.b + 1)
                        chain.done(v.tensor_scalar(xl[:, 0, :], xs[:, s, 0, :], mv[:, 0, 0:1], rstd[:, 0:1], ALU.subtract, ALU.mult))
                        v.tensor_scalar(xl[:, 1, :], xs[:, s, 1, :], mv[:, 1, 0:1], rstd[:, 1:2], ALU.subtract, ALU.mult).then_inc(xl_done, 1)
                        v.wait_ge(xl_done, p.b + 1)
                        chain.done(v.scalar_tensor_tensor(xl[:, 0, :], xl[:, 0, :], inv[:, 0:1], nw[:, :], ALU.mult, ALU.mult))
                        v.scalar_tensor_tensor(xl[:, 1, :], xl[:, 1, :], inv[:, 1:2], nw[:, :], ALU.mult, ALU.mult).then_inc(xn_done, 1)
                    if k:
                        s = k.slot(2)
                        chain.restart()
                        if n == 0:
                            hold(v, sim_done, (k.b + 1) * 4, vpass)
                        if n < len(FIRST):
                            for q in range(*FIRST[n]):
                                row = sim[:, s, q // SETS, (q % SETS) * KEYS:(q % SETS + 1) * KEYS]
                                chain.done(v.max(val[:, q, :], row))
                                chain.done(v.max_index(idx[:, q, :], val[:, q, :], row))
                        if n == 4:
                            v.sem_inc(val_done, 1)
                            chain.done(v.tensor_copy(idxf[:, :, :], idx[:, :, :]))
                            both = val[:, :, :].rearrange("p (s a) k -> p s a k", a=2)
                            chain.done(v.tensor_tensor(cand[:, :, :].rearrange("p s (a b) -> p s a b", a=PK),
                                                       both[:, :, 0, :].unsqueeze(3).broadcast_to((T, 2 * PH, PK, PK)),
                                                       both[:, :, 1, :].unsqueeze(2).broadcast_to((T, 2 * PH, PK, PK)), ALU.add))
                        if n in (4, 5):
                            for q in range((n - 4) * PH, (n - 3) * PH):
                                chain.done(v.max(best[:, q, :], cand[:, q, :]))
                                chain.done(v.max_index(ci[:, q, :], best[:, q, :], cand[:, q, :]))
                        if n == 5:
                            chain.done(v.tensor_scalar(cab[:, 0], ci[:, :, :], 3, None, ALU.logical_shift_right))
                            chain.done(v.tensor_scalar(cab[:, 1], ci[:, :, :], 7, None, ALU.bitwise_and))
                            chain.done(v.tensor_copy(cabf[:, :, :, :], cab[:, :, :, :]))
                            for half in range(2):
                                ins = v.tensor_tensor(eq[:, half], iota[0:T, 0:8].unsqueeze(1).unsqueeze(1).broadcast_to((T, 2 * PH, PK, 8)),
                                                      cabf[:, half].unsqueeze(3).broadcast_to((T, 2 * PH, PK, 8)), ALU.is_equal)
                            ins.then_inc(best_done, 1)
                    if k and n == GO - 1:
                        chain.restart()
                        v.wait_ge(ij_done, k.b + 1)
                        chain.done(v.reduce_sum(ij[:, :, :].rearrange("p a s -> p (a s)"), eq[:, :, :, :, :].rearrange("p a s k n -> p (a s k) n"), axis=X_AXIS))
                        chain.done(v.scalar_tensor_tensor(ef[:, :], ij[:, 0, :], float(KEYS), ij[:, 1, :], ALU.mult, ALU.add))
                        chain.done(v.tensor_copy(ei[:, 0, :], ef[:, :]))
                        chain.done(v.tensor_scalar(ei[:, 1, :], ei[:, 0, :], NC - 1, None, ALU.bitwise_and))
                        chain.done(v.tensor_scalar(ei[:, 0, :], ei[:, 0, :], NC.bit_length() - 1, None, ALU.logical_shift_right))
                        chain.done(v.tensor_scalar(kin[:, 2, :], best[:, :, :].rearrange("p s k -> p (s k)"), 0.0, None, ALU.max))
                        v.tensor_copy(kin[:, 0:2, :], ei[:, :, :]).then_inc(kin_done, 1)
                    if up and n == GO - 1:
                        s = up.slot(2)
                        v.wait_ge(xr_in[s], 16 * (up.round(2) + 1))
                        v.wait_ge(y_ps, up.b + 1)
                        v.scalar_tensor_tensor(y[:, s, :, :].rearrange("p t d -> p (t d)"), bU[0:T, :], tg[:, 3:4],
                                               y[:, s, :, :].rearrange("p t d -> p (t d)"), ALU.mult, ALU.add).then_inc(y_done, 1)
                    if w:
                        if n == 0:
                            v.wait_ge(g_done, (w.b + 1) * 2 * GO)
                        at_n = w.b * GO + n
                        v.wait_ge(w_ps, at_n + 1)
                        for half in range(2):
                            first = n * TG + half * TG // 2
                            here = g[:, w.slot(2)].rearrange("p c (t n) -> p t c n", t=2)[:, :, :, first:first + TG // 2]
                            ins = v.tensor_tensor(here, wbank[n % 2][:, half, 0:TG * NC].rearrange("p (n t c) -> p t c n", t=2, c=NC), here, ALU.mult)
                        ins.then_inc(w_done, 1)
                if k:
                    free(v, hc_done, k.b * GO)
                    v.wait_ge(kt_ps, k.b + 1)
                    chain.done(v.tensor_copy(pc[:, :, :].rearrange("p n t -> p (n t)"), bM[:, 0:2 * T]))
                    chain.done(v.tensor_copy(rp[:, :, 0], bM[:, 2 * T:3 * T]))
                    chain.done(v.tensor_tensor(rrest[:, :], bM[:, 2 * T:3 * T], rp[:, :, 0], ALU.subtract))
                    chain.done(v.tensor_copy(rp[:, :, 1], rrest[:, :]))
                    v.tensor_tensor(rp[:, :, 2], rrest[:, :], rp[:, :, 1], ALU.subtract).then_inc(kt_done, 1)
                    one_hot(k.b, 0)

            pipeline(v, PAIR, (0, 1, 2, 3), PEEL, step)

        @block.tensor
        def _(pe):
            pe.wait_ge(w_in, 112)
            for h in range(DH):
                for q in range(SETS):
                    mm = pe.matmul(wbank[h][:, q // 8, (q % 8) * KEYS:(q % 8 + 1) * KEYS], wq_s[:, q, h * 128:(h + 1) * 128], ks[:, q, :],
                                   start=True, stop=True)
            mm.then_inc(cset_ps, 1)
            pe.wait_ge(cset_done, 1)

            def step(p, k, w, up):
                for n in range(GO):
                    if up:
                        s = up.slot(2)
                        if n == 0:
                            pe.wait_ge(w_done, (up.b + 1) * GO)
                            free(pe, y_done, up.b)
                        for c in range(n * CG, (n + 1) * CG):
                            for h in range(DH):
                                mm = pe.matmul(bU[:, h * 2 * T:(h + 1) * 2 * T], u_s[:, c, h * 128:(h + 1) * 128], g[:, s, c, :],
                                               start=c == 0 and h == 0, stop=c == NC - 1 and h == DH - 1)
                        if n == GO - 1:
                            mm.then_inc(u_ps, 1)
                    for u in range(2):
                        if k:
                            s = k.slot(2)
                            at_u = (k.b * GO + n) * 2 + u
                            if n == 0 and u == 0:
                                pe.wait_ge(xnT_done, k.b + 1)
                            free(pe, g_done, at_u - 1)
                            for cc in range(2):
                                c = n * CG + 2 * u + cc
                                for h in range(DH):
                                    mm = pe.matmul(bD[u][:, cc * 2 * T:(cc + 1) * 2 * T], dT[:, h, c, :], xnT[:, s, h, :], start=h == 0, stop=h == DH - 1)
                            mm.then_inc(d_ps, 1)
                    if up and n == GO - 1:
                        pe.wait_ge(oT_done, up.b + 1)
                        for t in range(2):
                            for h in range(DH):
                                mm = pe.transpose(bU[0:T, (t * DH + h) * 128:(t * DH + h + 1) * 128], oT[:, h, t * T:(t + 1) * T], ident)
                        mm.then_inc(y_ps, 1)
                    if w:
                        at_n = w.b * GO + n
                        pe.wait_ge(hp_done, at_n + 1)
                        pe.wait_ge(hc_done, at_n + 1)
                        free(pe, w_done, at_n - 1)
                        for tok in range(TG):
                            half, place = tok // (TG // 2), tok % (TG // 2)
                            for part in range(3):
                                mm = pe.matmul(wbank[n % 2][:, half, place * 2 * NC:(place + 1) * 2 * NC], hotp[:, n % 2, tok, :],
                                               hotw[:, n % 2, tok, part, :], start=part == 0, stop=part == 2)
                        mm.then_inc(w_ps, 1)
                    if p and n == 2:
                        pe.wait_ge(xn_done, p.b + 1)
                        free(pe, kt_done, p.b - 1)
                        free(pe, sim_done, p.b * 4)
                        for h in range(DH):
                            for t in range(2):
                                mm = pe.transpose(bM[:, (h * 2 + t) * T:(h * 2 + t + 1) * T], xl[:, t, h * 128:(h + 1) * 128], ident[0:T, 0:T])
                        mm.then_inc(xt_ps, 1)
                    if p and 3 <= n < 7:
                        q = n - 3
                        if q == 0:
                            pe.wait_ge(xnT_done, p.b + 1)
                        free(pe, sim_done, p.b * 4 + q)
                        for h in range(DH):
                            mm = pe.matmul(bM[0:T, 0:512], xnT[:, p.slot(2), h, (q // 2) * T:(q // 2 + 1) * T],
                                           cw[:, h, (q % 2) * 512:(q % 2 + 1) * 512], start=h == 0, stop=h == DH - 1)
                        mm.then_inc(sim_ps, 1)
                if k:
                    pe.wait_ge(kin_done, k.b + 1)
                    pe.wait_ge(sim_done, upto((k.b + 2) * 4, PAIR * 4))
                    for part in range(3):
                        mm = pe.transpose(bM[:, part * T:(part + 1) * T], kin[:, part, :], ident[0:T, 0:T])
                    mm.then_inc(kt_ps, 1)

            pipeline(pe, PAIR, (0, 1, 2, 3), PEEL, step)

        work.close()
        at_rest(nc, signals)




DEBUG = False
_OUTS = [((B, T, D), "float32")]


def kernel(**inputs):
    import numpy as np
    import concourse.bacc as _bacc
    from concourse import mybir as _mybir
    from concourse.bass_utils import run_bass_kernel_spmd as _run

    I = inputs
    rows = lambda a: np.ascontiguousarray(np.broadcast_to(a, (T, a.shape[-1])))
    lay = {
        "x": I["x"], "ctxT": I["ctx_1024"].transpose(0, 2, 1),
        "wq": I["L0_xattn_Wq"], "wk": I["L0_xattn_Wk"], "wv": I["L0_xattn_Wv"], "wp": I["L0_xattn_Wp"],
        "bp": rows(I["L0_xattn_bp"]), "wg": I["L0_ffn_Wg"].T,
        "w1": I["L0_ffn_W1"], "w2": I["L0_ffn_W2"],
        "ctx": I["ctx_1024"], "wqc": I["L1_xattn_Wq_c"], "wks": I["L1_xattn_Wk_s"], "wkc": I["L1_xattn_Wk_c"], "wqs": I["L1_xattn_Wq_s"],
        "wvsT": I["L1_xattn_Wv_s"].T, "wvcT": I["L1_xattn_Wv_c"].T, "wgT": I["L1_xattn_Wg"].T,
        "bcols": np.stack([I["L1_xattn_bq_c"], I["L1_xattn_bk_s"], I["L1_xattn_bk_c"], I["L1_xattn_bq_s"]], axis=1),
        "brows": np.broadcast_to(np.stack([I["L1_xattn_bv_s"], I["L1_xattn_bv_c"], I["L1_xattn_bg"]]), (T, 3, D)),
        "pwq": I["L1_ffn_w_q"], "keysT": I["L1_ffn_keys"].transpose(3, 0, 2, 1).reshape(DK, SETS, KEYS),
        "downT": I["L1_ffn_expert_down"].reshape(128, NC, D).transpose(2, 1, 0), "up": I["L1_ffn_expert_up"],
        "norm": rows(I["L1_ffn_norm_w"]),
        "gates": rows(np.concatenate([I["g_xattn"], I["g_ffn"]])),
    }
    consts = np.zeros((128, 512), np.float32)
    consts[:, 0:128] = np.eye(128)
    consts[0:T, 128:128 + T] = np.triu(np.ones((T, T)), 1)
    consts[:, 240:240 + T] = 1.0
    consts[:, 352:480] = np.arange(128)
    where = np.clip((np.arange(T, dtype=np.float32) + np.float32(0.5)) * np.float32(M / T) - np.float32(0.5), 0, M - 1).astype(np.float32)
    low = np.floor(where).astype(np.int64)
    share = where - low.astype(np.float32)
    weight = np.zeros((M, T), np.float32)
    weight[low, np.arange(T)] += 1 - share
    weight[np.minimum(low + 1, M - 1), np.arange(T)] += share
    lay["interp"] = weight.reshape(KT, KP, T).transpose(1, 0, 2)
    lay["consts"] = consts
    nc = _bacc.Bacc("TRN2", target_bir_lowering=False, num_devices=1)
    arrays, aps = {}, {}
    for name, a in lay.items():
        a = np.ascontiguousarray(a)
        arrays[f"in_{name}"] = a
        aps[name] = nc.dram_tensor(f"in_{name}", a.shape, _mybir.dt.from_np(a.dtype), kind="ExternalInput").ap()
    K = "ExternalOutput"
    def scratch(name, shape, dt=F32, debug=False):
        return nc.dram_tensor(name, shape, dt, kind="ExternalOutput" if debug else "Internal").ap()
    x1_d = scratch("x1_d", (B, T, D), debug=DEBUG)
    disp_d = scratch("disp_d", (E * CAP, D), debug=DEBUG)
    slot_d = scratch("slot_d", (B, T, 2), I32, debug=DEBUG)
    gate_d = scratch("gate_d", (B, T, 2), debug=DEBUG)
    kst_d = [scratch(f"kstage{s}", (3 * D, M), BF16) for s in range(2)]
    qst_d = [scratch(f"qstage{s}", (3 * D, T), BF16) for s in range(2)]
    mst_d = [scratch(f"mstage{s}", (H, 3 * T), BF16) for s in range(2)]
    attend(nc, aps["x"], aps["ctxT"], aps["wq"], aps["wk"], aps["wv"], aps["wp"], aps["bp"], aps["wg"], aps["gates"], aps["consts"],
           x1_d, disp_d, slot_d, gate_d, kst_d, qst_d, mst_d)
    eout_d = scratch("eout_d", (E * CAP, D), debug=DEBUG)
    experts(nc, aps["w1"], aps["w2"], aps["consts"], disp_d, eout_d)
    x3_d = scratch("x3_d", (B, T, D), debug=DEBUG)
    cross(nc, x1_d, eout_d, slot_d, gate_d, aps["ctxT"], aps["ctx"], aps["wqc"], aps["wks"], aps["wkc"], aps["wqs"], aps["wvsT"], aps["wvcT"],
          aps["wgT"], aps["bcols"], aps["brows"], aps["gates"], aps["consts"], aps["interp"], None, x3_d)
    out_d = nc.dram_tensor("out_0", (B, T, D), F32, kind="ExternalOutput").ap()
    retrieve(nc, x3_d, aps["pwq"], aps["keysT"], aps["downT"], aps["up"], aps["norm"], aps["gates"], aps["consts"], out_d)
    r = _run(nc, [arrays], core_ids=[0])
    return r.results[0]["out_0"]
```
